# Optimizing a Trainium2 kernel written in Bass

```python
import numpy as np
import jax
import jax.numpy as jnp

def _softmax(x, axis=-1):
    return jax.nn.softmax(x, axis=axis)

def _gelu(x):
    return jax.nn.gelu(x, approximate=True)

def _silu(x):
    return jax.nn.silu(x)

def _sigmoid(x):
    return jax.nn.sigmoid(x)

def _layernorm(x, axis=-1, eps=1e-05):
    m = jnp.mean(x, axis=axis, keepdims=True)
    v = jnp.var(x, axis=axis, keepdims=True)
    return (x - m) / jnp.sqrt(v + eps)

def _scatter_add(tgt, idx, src, axis=0):
    return tgt.at[idx].add(src)

def _segment_sum(src, seg, n):
    return jax.ops.segment_sum(src, seg, n)
kernel_name = 'mk_seq_postln_d1_jaxref_r2_fc9136'

def setup_inputs(seed: int=0):
    np.random.seed(seed)
    _w = jnp.asarray

    def _L0_attn_setup():
        import jax, jax.numpy as jnp
        import numpy as np
        import math
        D_MODEL = 512
        N_HEADS = 16
        D_HEAD = D_MODEL // N_HEADS
        LSR_RANK = 32
        B, T = (4, 1024)
        key = jax.random.key(seed)
        ks = jax.random.split(key, 11)
        s = 1.0 / math.sqrt(D_MODEL)
        x = jax.random.normal(ks[0], (B, T, D_MODEL), dtype=jnp.float32)
        Wq = jax.random.uniform(ks[1], (D_MODEL, D_MODEL), minval=-s, maxval=s)
        bq = jax.random.uniform(ks[2], (D_MODEL,), minval=-s, maxval=s)
        Wk = jax.random.uniform(ks[3], (D_MODEL, D_MODEL), minval=-s, maxval=s)
        bk = jax.random.uniform(ks[4], (D_MODEL,), minval=-s, maxval=s)
        Wv = jax.random.uniform(ks[5], (D_MODEL, D_MODEL), minval=-s, maxval=s)
        bv = jax.random.uniform(ks[6], (D_MODEL,), minval=-s, maxval=s)
        Wo = jax.random.uniform(ks[7], (D_MODEL, D_MODEL), minval=-s, maxval=s)
        bo = jax.random.uniform(ks[8], (D_MODEL,), minval=-s, maxval=s)
        Wq_lsr = jax.random.normal(ks[9], (N_HEADS, D_HEAD, LSR_RANK)) / math.sqrt(D_HEAD)
        Wk_lsr = jax.random.normal(ks[10], (N_HEADS, D_HEAD, LSR_RANK)) / math.sqrt(D_HEAD)
        return {'x': x, 'Wq': Wq, 'bq': bq, 'Wk': Wk, 'bk': bk, 'Wv': Wv, 'bv': bv, 'Wo': Wo, 'bo': bo, 'Wq_lsr': Wq_lsr, 'Wk_lsr': Wk_lsr}
    _L0_attn_in = _L0_attn_setup()

    def _L0_ffn_setup():
        import jax, jax.numpy as jnp
        import numpy as np
        import math
        B, L, D = (4, 2048, 512)
        F = 2048
        E = 16
        CAP_FACTOR = 1.0
        EPS = 1e-05
        key = jax.random.key(seed)
        ks = jax.random.split(key, 8)
        std = 0.02
        return {'x': jax.random.normal(ks[0], (B, L, D), dtype=jnp.float32), 'norm_weight': jnp.ones((D,), dtype=jnp.float32), 'router_weight': jax.random.normal(ks[1], (E, D), dtype=jnp.float32) * std, 'router_bias': jnp.zeros((E,), dtype=jnp.float32), 'fc1_weight': jax.random.normal(ks[2], (E, F, D), dtype=jnp.float32) * std, 'fc1_bias': jnp.zeros((E, F), dtype=jnp.float32), 'fc2_weight': jax.random.normal(ks[3], (E, D, F), dtype=jnp.float32) * std, 'fc2_bias': jnp.zeros((E, D), dtype=jnp.float32)}
    _L0_ffn_in = _L0_ffn_setup()
    _d = {'L0_attn_x': _L0_attn_in['x'], 'L0_attn_Wq': _L0_attn_in['Wq'], 'L0_attn_bq': _L0_attn_in['bq'], 'L0_attn_Wk': _L0_attn_in['Wk'], 'L0_attn_bk': _L0_attn_in['bk'], 'L0_attn_Wv': _L0_attn_in['Wv'], 'L0_attn_bv': _L0_attn_in['bv'], 'L0_attn_Wo': _L0_attn_in['Wo'], 'L0_attn_bo': _L0_attn_in['bo'], 'L0_attn_Wq_lsr': _L0_attn_in['Wq_lsr'], 'L0_attn_Wk_lsr': _L0_attn_in['Wk_lsr'], 'L0_ffn_norm_weight': _L0_ffn_in['norm_weight'], 'L0_ffn_router_weight': _L0_ffn_in['router_weight'], 'L0_ffn_router_bias': _L0_ffn_in['router_bias'], 'L0_ffn_fc1_weight': _L0_ffn_in['fc1_weight'], 'L0_ffn_fc1_bias': _L0_ffn_in['fc1_bias'], 'L0_ffn_fc2_weight': _L0_ffn_in['fc2_weight'], 'L0_ffn_fc2_bias': _L0_ffn_in['fc2_bias']}
    _x0 = _d['L0_attn_x']
    _d['L0_attn_x'] = jax.random.normal(jax.random.fold_in(jax.random.key(seed), 1), (8, 1024, 512), dtype=_x0.dtype)
    del _x0
    return _d

def reference(L0_attn_x, L0_attn_Wq, L0_attn_bq, L0_attn_Wk, L0_attn_bk, L0_attn_Wv, L0_attn_bv, L0_attn_Wo, L0_attn_bo, L0_attn_Wq_lsr, L0_attn_Wk_lsr, L0_ffn_norm_weight, L0_ffn_router_weight, L0_ffn_router_bias, L0_ffn_fc1_weight, L0_ffn_fc1_bias, L0_ffn_fc2_weight, L0_ffn_fc2_bias):

    def _L0_attn_ref(x, Wq, bq, Wk, bk, Wv, bv, Wo, bo, Wq_lsr, Wk_lsr):
        import jax, jax.numpy as jnp
        import numpy as np
        import math
        D_MODEL = 512
        N_HEADS = 16
        D_HEAD = D_MODEL // N_HEADS
        LSR_RANK = 32
        B, T = (4, 1024)
        Bq, Tq, _ = x.shape

        def split_heads(y):
            return y.reshape(Bq, Tq, N_HEADS, D_HEAD).transpose(0, 2, 1, 3)
        q = split_heads(x @ Wq.T + bq)
        k = split_heads(x @ Wk.T + bk)
        v = split_heads(x @ Wv.T + bv)
        q_lr = jnp.einsum('bhtd,hdr->bhtr', q, Wq_lsr)
        k_lr = jnp.einsum('bhtd,hdr->bhtr', k, Wk_lsr)
        scale = 1.0 / math.sqrt(max(LSR_RANK, 1))
        scores = jnp.einsum('bhir,bhjr->bhij', q_lr, k_lr) * scale
        causal_mask = jnp.triu(jnp.ones((Tq, Tq), dtype=bool), k=1)
        scores = jnp.where(causal_mask, jnp.float32(-jnp.inf), scores)
        attn = jax.nn.softmax(scores, axis=-1)
        y = jnp.einsum('bhij,bhjd->bhid', attn, v)
        y = y.transpose(0, 2, 1, 3).reshape(Bq, Tq, D_MODEL)
        return y @ Wo.T + bo

    def _L0_ffn_ref(x, norm_weight, router_weight, router_bias, fc1_weight, fc1_bias, fc2_weight, fc2_bias):
        import jax, jax.numpy as jnp
        import numpy as np
        import math
        B, L, D = (4, 2048, 512)
        F = 2048
        E = 16
        CAP_FACTOR = 1.0
        EPS = 1e-05
        b, l, d = x.shape
        n_tokens = b * l
        n_experts = router_weight.shape[0]
        capacity = max(1, math.ceil(CAP_FACTOR * n_tokens / n_experts))
        top_k = min(capacity, n_tokens)
        xf = x.reshape(n_tokens, d)
        rms = jnp.sqrt(jnp.mean(xf * xf, axis=-1, keepdims=True) + EPS)
        xn = xf / rms * norm_weight
        logits = xn @ router_weight.T + router_bias
        probs = jax.nn.softmax(logits, axis=-1)
        _, idx = jax.lax.top_k(logits.T, top_k)
        xe = xn[idx]
        h = jnp.einsum('ecd,efd->ecf', xe, fc1_weight) + fc1_bias[:, None, :]
        h = jax.nn.gelu(h, approximate=False)
        y = jnp.einsum('ecf,edf->ecd', h, fc2_weight) + fc2_bias[:, None, :]
        gates = jnp.take_along_axis(probs.T, idx, axis=1)
        flat_idx = idx.reshape(-1)
        contrib = (y * gates[:, :, None]).reshape(-1, d)
        output = jnp.zeros((n_tokens, d), dtype=x.dtype).at[flat_idx].add(contrib)
        gate_sums = jnp.zeros((n_tokens, 1), dtype=x.dtype).at[flat_idx].add(gates.reshape(-1, 1))
        assigned = gate_sums > 0
        output = jnp.where(assigned, output / jnp.where(assigned, gate_sums, 1.0), output)
        return output.reshape(b, l, d)
    x = L0_attn_x
    x = _layernorm(x + _L0_attn_ref(x, L0_attn_Wq, L0_attn_bq, L0_attn_Wk, L0_attn_bk, L0_attn_Wv, L0_attn_bv, L0_attn_Wo, L0_attn_bo, L0_attn_Wq_lsr, L0_attn_Wk_lsr), axis=-1)
    x = _layernorm(x + _L0_ffn_ref(x, L0_ffn_norm_weight, L0_ffn_router_weight, L0_ffn_router_bias, L0_ffn_fc1_weight, L0_ffn_fc1_bias, L0_ffn_fc2_weight, L0_ffn_fc2_bias), axis=-1)
    return x

_drawn_inputs = setup_inputs


def setup_inputs(seed=0):
    import zlib

    import numpy as np

    out = dict(_drawn_inputs(seed))
    spreads = {'L0_ffn_norm_weight': (1.0, 0.2),
     'L0_ffn_router_bias': (0.0, 0.8),
     'L0_ffn_fc1_bias': (0.0, 0.1),
     'L0_ffn_fc2_bias': (0.0, 0.1)}
    factors = {'L0_attn_bq': 34.506, 'L0_attn_bk': 64.0, 'L0_attn_bv': 3.304}
    for name, (base, spread) in spreads.items():
        noise = np.random.default_rng([zlib.crc32(name.encode()), seed]).standard_normal(out[name].shape)
        drawn = base * np.exp(spread * noise) if base else spread * noise
        out[name] = jnp.asarray(drawn.astype(out[name].dtype))
    for name, factor in factors.items():
        out[name] = (out[name] * factor).astype(out[name].dtype)
    return out
```

```python
from contextlib import ExitStack

import numpy as np
import concourse.bass as bass
from concourse import mybir

F32 = mybir.dt.float32
F32R = mybir.dt.float32r
BF16 = mybir.dt.bfloat16
I32 = mybir.dt.int32
U32 = mybir.dt.uint32
ALU = mybir.AluOpType
ACT = mybir.ActivationFunctionType
AX = mybir.AxisListType

P = 128
D = 512
DC = D // P
HEADS = 16
DH = 32
HG = P // DH
GROUPS = HEADS // HG
T = 1024
TT = T // P
HALF = 512
EPS = 1e-5
SCALE = 1.0 / float(np.sqrt(DH))
MASKED = -(2.0 ** 120)
HI, LO = 0, 1

Q_STRIPS = (HI, LO, HI)
K_STRIPS = (HI, HI, LO)
MAX_STRIP = 96


def raw(ap):
    return ap.bitcast(F32)


def plain(eng, semaphore, value, passed):
    eng.wait_ge(semaphore, value)
    eng.sem_inc(passed, 1)


def build_weights(nc, w, scratch, keep):
    with ExitStack() as ctx:
        sb = lambda name, shape, dt=F32: ctx.enter_context(nc.sbuf_tensor(name, shape, dt))
        sem = lambda name: ctx.enter_context(nc.semaphore(name))
        lq = sb("lq_blocks", [P, GROUPS, P])
        lk = sb("lk_blocks", [P, GROUPS, P])
        fold = sb("fold", [P, GROUPS, P])
        wq = sb("wq_rows", [P, GROUPS, D])
        wqf = sb("wq_folded", [P, GROUPS, DC, P])
        wk = sb("wk_cols", [P, DC, GROUPS, P])
        wv = sb("wv_cols", [P, DC, D])
        parts = sb("qk_parts", [P, GROUPS, 4, DC, P], F32R)
        bq = sb("bq_cols", [P, GROUPS])
        bv = sb("bv_cols", [P, GROUPS])
        bv_wide = sb("bv_wide", [P, GROUPS, P])
        bo = sb("bo_rows", [P, D])
        ones = sb("setup_ones", [P, P])
        ps_fold = ctx.enter_context(nc.psum_tensor("ps_fold", [P, GROUPS, P], F32))
        ps_wq = ctx.enter_context(nc.psum_tensor("ps_wq", [P, GROUPS, DC * P], F32))
        ps_bias = ctx.enter_context(nc.psum_tensor("ps_bias", [P, HALF], F32))
        ps_bo = ctx.enter_context(nc.psum_tensor("ps_bo", [P, D], F32))
        zeroed, blocks_in, in_q, in_rest = sem("zeroed"), sem("blocks_in"), sem("in_q"), sem("in_rest")
        fold_mm, folded, wq_mm, bias_done = sem("fold_mm"), sem("folded"), sem("wq_mm"), sem("bias_done")
        copied, split_hi, split_lo, stored = sem("copied"), sem("split_hi"), sem("split_lo"), sem("stored")
        wide, bo_mm = sem("wide"), sem("bo_mm")
        block = ctx.enter_context(nc.Block())

        @block.sync
        def _(sp):
            sp.dma_start(wq[:], w["Wq"].rearrange("(g p) d -> p g d", p=P)).then_inc(in_q, 16)
            with nc.allow_non_contiguous_dma(reason="small bias columns"):
                sp.dma_start(bq[:], w["bq"].rearrange("(g p) -> p g", p=P)).then_inc(in_q, 16)
                sp.dma_start(bv[:], w["bv"].rearrange("(g p) -> p g", p=P)).then_inc(in_rest, 16)
                sp.dma_start(keep["bk"][:], w["bk"].rearrange("(g p) -> p g", p=P)).then_inc(in_rest, 16)
            sp.dma_start(bo[:], w["bo"].rearrange("(a n) -> a n", a=1).to_broadcast([P, D])).then_inc(in_rest, 16)
            sp.dma_start(wk[:], w["WkT"].rearrange("(c p) (g n) -> p c g n", p=P, n=P)).then_inc(in_rest, 16)
            sp.dma_start(wv[:], w["WvT"].rearrange("(c p) n -> p c n", p=P)).then_inc(in_rest, 16)
            sp.dma_start(keep["wo"][:], w["WoT"].rearrange("(c p) n -> p c n", p=P)).then_inc(in_rest, 16)
            sp.wait_ge(zeroed, 2)
            for h in range(HEADS):
                g, r = h // HG, DH * (h % HG)
                sp.dma_start(lq[r:r + DH, g, r:r + DH], w["LqT"][h]).then_inc(blocks_in, 16)
                sp.dma_start(lk[r:r + DH, g, r:r + DH], w["LkT"][h]).then_inc(blocks_in, 16)
            sp.wait_ge(split_hi, 2)
            sp.wait_ge(split_lo, 2)
            sp.dma_start(scratch["wqk"].rearrange("g p k -> p g k"),
                         raw(parts[:]).rearrange("p g k c n -> p g (k c n)")).then_inc(stored, 16)
            sp.wait_ge(stored, 16)

        @block.gpsimd
        def _(pool):
            pool.memset(lq[:], 0.0).then_inc(zeroed, 1)
            pool.memset(lk[:], 0.0).then_inc(zeroed, 1)

        @block.tensor
        def _(pe):
            pe.wait_ge(blocks_in, 16 * 2 * HEADS)
            for g in range(GROUPS):
                mm = pe.matmul(ps_fold[:, g, :], lq[:, g, :], lk[:, g, :], start=True, stop=True)
            mm.then_inc(fold_mm, 1)
            pe.wait_ge(folded, 1)
            pe.wait_ge(in_q, 32)
            for g in range(GROUPS):
                for c in range(DC):
                    mm = pe.matmul(ps_wq[:, g, c * P:(c + 1) * P], wq[:, g, c * P:(c + 1) * P], fold[:, g, :],
                                   start=True, stop=True)
                mm.then_inc(wq_mm, 1)
            for g in range(GROUPS):
                mm = pe.matmul(ps_bias[:, g:g + 1], fold[:, g, :], bq[:, g:g + 1], start=True, stop=True)
            mm.then_inc(bias_done, 1)
            pe.wait_ge(wide, 2)
            pe.wait_ge(in_rest, 96)
            for c in range(DC):
                mm = pe.matmul(ps_bo[:], bv_wide[:, c, :], keep["wo"][:, c, :], start=(c == 0), stop=(c == DC - 1))
            mm.then_inc(bo_mm, 1)

        @block.vector
        def _(dve):
            dve.wait_ge(fold_mm, 1)
            dve.tensor_copy(fold[:], ps_fold[:]).then_inc(folded, 1)
            for g in range(GROUPS):
                dve.wait_ge(wq_mm, g + 1)
                dve.tensor_copy(wqf[:, g], ps_wq[:, g, :].rearrange("p (c n) -> p c n", c=DC)).then_inc(copied, 1)
            dve.wait_ge(bias_done, 1)
            dve.tensor_copy(keep["bq"][:], ps_bias[:, 0:GROUPS]).then_inc(copied, 1)
            dve.memset(ones[:], 1.0).then_inc(wide, 1)
            dve.wait_ge(wide, 1)
            dve.wait_ge(in_rest, 96)
            for g in range(GROUPS):
                ins = dve.tensor_scalar(bv_wide[:, g, :], ones[:], bv[:, g:g + 1], None, ALU.mult)
            ins.then_inc(wide, 1)
            dve.wait_ge(copied, GROUPS + 1)
            dve.tensor_copy(parts[:, :, 0], wqf[:]).then_inc(split_hi, 1)
            dve.tensor_copy(parts[:, :, 2], wk[:].rearrange("p c g n -> p g c n")).then_inc(split_hi, 1)
            dve.tensor_copy(keep["wv"][:, HI], wv[:]).then_inc(split_hi, 1)
            dve.wait_ge(split_hi, 3)
            for g in range(GROUPS):
                dve.tensor_tensor(parts[:, g, 1], wqf[:, g], raw(parts[:, g, 0]), ALU.subtract)
                ins = dve.tensor_tensor(parts[:, g, 3], wk[:, :, g, :], raw(parts[:, g, 2]), ALU.subtract)
            ins.then_inc(split_lo, 2)
            dve.tensor_tensor(keep["wv"][:, LO], wv[:], raw(keep["wv"][:, HI]), ALU.subtract).then_inc(split_lo, 1)
            dve.wait_ge(bo_mm, 1)
            dve.tensor_tensor(keep["bo"][:], ps_bo[:], bo[:], ALU.add).then_inc(split_lo, 1)


def plan_batch():
    order = [("v", t) for t in range(TT)]
    for g in range(GROUPS):
        order += plan_step(g, True)
    order += [("out", t) for t in range(TT)]
    return order


def attend_steps():
    return [(hh, j, max(0, j * P - hh * HALF)) for hh in range(2) for j in range(4 * hh + 4)]


def max_steps():
    out = []
    for h in range(HG):
        out += [(h, it, it, 0, (it + 1) * P) for it in range(4)]
        out += [(h, it, it, 0, HALF) for it in range(4, TT)]
        out += [(h, it + 4, it, HALF, (it + 1) * P - HALF) for it in range(4, TT)]
    return out


PROB_BUFS = 4
LEAD = 2
TAIL = 1


def attend_parts(g, k, e):
    parts = [("scores", g, k, 0), ("scores", g, k, 1)]
    for n in ([k - 1] if k > 0 else []) + ([k] if k == e - 1 else []):
        parts += [("values", g, n), ("sums", g, n)]
    return parts


def plan_step(g, attend):
    order = [("proj", g, i) for i in range(4)]
    e, m = len(attend_steps()) if attend else 0, len(max_steps())
    if not attend:
        return order + [("max", g, i) for i in range(m)] + [("maxT", g)]
    spots = sum(len(attend_parts(g, k, e)) for k in range(LEAD, e - TAIL))
    done = spot = 0
    for k in range(e):
        for part in attend_parts(g, k, e):
            order.append(part)
            if LEAD <= k < e - TAIL:
                spot += 1
                share = m * spot // spots
                order += [("max", g, i) for i in range(done, share)]
                done = share
        if k == e - TAIL - 1:
            order.append(("maxT", g))
    assert done == m
    return order


def build_attention(nc, x_dram, xT_dram, x1_dram, scratch, keep, NB):
    with ExitStack() as ctx:
        sb = lambda name, shape, dt=F32: ctx.enter_context(nc.sbuf_tensor(name, shape, dt))
        ps = lambda name, shape, dt=F32: ctx.enter_context(nc.psum_tensor(name, shape, dt))
        sem = lambda name: ctx.enter_context(nc.semaphore(name))

        xs = sb("x_parts", [P, 2, DC, T], F32R)
        wqk = sb("wqk_group", [P, 4, DC, P], F32R)
        nat = sb("natural", [P, 4, T])
        q_ops = sb("q_operands", [P, 2, HG, T], F32R)
        k_ops = sb("k_operands", [P, 2, HG, T], F32R)
        v = sb("v_rows", [P, TT, D])
        y = sb("y_cols", [P, GROUPS, T])
        probs = sb("probs", [P, PROB_BUFS, 2, HALF])
        mx = sb("max_slots", [P, HG, 12])
        mrow = sb("row_max", [P, HG, TT])
        mneg = sb("minus_max", [HG * TT, 2, P], F32R)
        rden = sb("rden", [P, HALF])
        xres = sb("x_residual", [P, 2, D])
        x1 = sb("x1_tile", [P, 2, D])
        stats = sb("ln_stats", [P, TT, 6])
        mv = sb("ln_mv", [P, 2, 2])
        std = sb("ln_std", [P, 2])
        rstd = sb("ln_rstd", [P, 2])
        eps = sb("eps_tile", [P, 1])
        ones = sb("ones_f32", [P, DH])
        ident = sb("ident_f32", [P, P])
        identb = sb("ident_bf16", [P, P], BF16)
        mask_q = sb("mask_q_rows", [P, P], BF16)
        mask_k = sb("mask_k_rows", [P, P], BF16)

        shared = ps("shared_banks", [P, 2, HALF])
        st = ps("scores_t", [P, 2, 2, HALF])
        yb = ps("y_bank", [P, HALF])
        db = ps("den_bank", [P, HALF])

        bank_full = [sem(f"bank{k}_full") for k in range(2)]
        bank_free = [sem(f"bank{k}_free") for k in range(2)]
        consts, strip_zero, own_zeros, ident_ready = sem("consts"), sem("strip_zero"), sem("own_zeros"), sem("ident_ready")
        x_in, x_split, w_in = sem("x_in"), sem("x_split"), sem("w_in")
        hi_ready = sem("hi_ready")
        sp_passed, pool_passed, dve_passed = sem("sp_passed"), sem("pool_passed"), sem("dve_passed")
        strips_sent = [sem(f"strips_sent{h}") for h in range(HG)]
        st_full, exp_done, pv_done, normed = sem("st_full"), sem("exp_done"), sem("pv_done"), sem("normed")
        rden_ready = sem("rden_ready")
        mx_joined, mneg_hi, m_sent = sem("mx_joined"), sem("mneg_hi"), sem("m_sent")
        res_in, x1_out = [sem(f"res_in{r}") for r in range(2)], [sem(f"x1_out{r}") for r in range(2)]
        bo_added, summed, stats_ready, mv_ready, std_ready, rstd_ready, x1_ready = (
            sem("bo_added"), sem("summed"), sem("stats_ready"), sem("mv_ready"), sem("std_ready"),
            sem("rstd_ready"), sem("x1_ready"))

        N_CONSTS = 8
        STRIPS = 16 * 2 * len(Q_STRIPS)
        steps, maxes = attend_steps(), max_steps()
        NE, NM = len(steps), len(maxes)
        batch = plan_batch()
        lead_in = plan_step(GROUPS - 1, False)
        uses_bank = lambda item: item[0] not in ("scores", "values", "sums")
        N_LEAD = sum(map(uses_bank, lead_in))
        N_BATCH = sum(map(uses_bank, batch))
        N_LAST = N_BATCH - 4 - NM - 1
        assert N_BATCH % 2 == 0

        def slot_of(k, pair):
            return (2 * k + pair) % PROB_BUFS

        assert PROB_BUFS == 4 and (2 * NE) % PROB_BUFS == 0

        def turns(order, base):
            at, n = {}, base
            for item in order:
                if uses_bank(item):
                    at[item] = (n % 2, n // 2)
                    n += 1
            return at

        lead_turns = turns(lead_in, 0)
        batch_turns = turns(batch, N_LEAD)
        last = [i for i in batch if not (i[0] in ("proj", "max", "maxT") and i[1] == GROUPS - 1)]
        last_turns = turns(last, N_LEAD)

        def scope(b, lead=False):
            if lead:
                return lead_in, lead_turns, 0
            if isinstance(b, int) and b == NB - 1:
                return last, last_turns, b * (N_BATCH // 2)
            return batch, batch_turns, b * (N_BATCH // 2)

        def await_parts(eng, passed, b, g, lead=False):
            _, at, off = scope(b, lead)
            for i in (2, 3):
                bank, turn = at[("proj", g, i)]
                plain(eng, bank_free[bank], off + turn + 1, passed)

        def each_batch(eng, run):
            if NB > 1:
                with eng.Fori(0, NB - 1) as b:
                    run(b)
            run(NB - 1)

        block = ctx.enter_context(nc.Block())

        @block.sync
        def _(sp):
            def load_x(b, n):
                for h in range(HG):
                    sp.wait_ge(strips_sent[h], n * STRIPS)
                sp.dma_start(nat[:], xT_dram.rearrange("(c p) t -> p c t", p=P)[:, :, bass.ds(b * T, T)]
                             ).then_inc(x_in, 16)

            def load_w(g):
                sp.dma_start(raw(wqk[:]), scratch["wqk"][g].rearrange("p (k c n) -> p k c n", k=4, c=DC)).then_inc(w_in, 16)

            def strips(b, g, lead=False):
                await_parts(sp, sp_passed, b, (g - 1) % GROUPS, lead)
                for h in range(HG):
                    src = slice(DH * h, DH * h + DH)
                    for s in range(3):
                        dst = slice(DH * s, DH * s + DH)
                        sp.dma_start(raw(q_ops[dst, g % 2, h, :]), nat[src, Q_STRIPS[s], :]).then_inc(strips_sent[h], 16)
                        sp.dma_start(raw(k_ops[dst, g % 2, h, :]), nat[src, 2 + K_STRIPS[s], :]).then_inc(strips_sent[h], 16)

            def run(b):
                n0 = b * GROUPS
                more = not (isinstance(b, int) and b == NB - 1)
                for g in range(GROUPS - 1):
                    load_w(g + 1)
                    strips(b, g + 1)
                if more:
                    load_x(b + 1, n0 + GROUPS)
                    load_w(0)
                    strips(b, 0)
                for t in range(TT):
                    sp.wait_ge(summed, b * TT + max(t - 1, 0))
                    sp.dma_start(xres[:, t % 2], x_dram[bass.ds(b * T + t * P, P), :]).then_inc(res_in[t % 2], 16)
                    if t >= 2:
                        store(b, t - 2)
                store(b, TT - 2)
                store(b, TT - 1)

            def store(b, t):
                sp.wait_ge(x1_ready, b * TT + t + 1)
                sp.dma_start(x1_dram[bass.ds(b * T + t * P, P), :], x1[:, t % 2]).then_inc(x1_out[t % 2], 16)

            load_x(0, 0)
            load_w(0)
            strips(0, 0, True)
            each_batch(sp, run)
            for r in range(2):
                sp.wait_ge(x1_out[r], 16 * TT // 2 * NB)

        @block.gpsimd
        def _(pool):
            pool.memset(eps[:], EPS).then_inc(consts, 1)
            pool.memset(ones[:], 1.0).then_inc(consts, 1)
            pool.memset(ident[:], 0.0).then_inc(own_zeros, 1)
            pool.memset(mask_q[:], 0.0).then_inc(own_zeros, 1)
            pool.memset(mask_k[:], 0.0).then_inc(own_zeros, 1)
            pool.wait_ge(own_zeros, 3)
            pool.affine_select(out=ident[:], in_=ident[:], compare_op=ALU.not_equal, fill=1.0, base=0,
                               pattern=[[-1, P]], channel_multiplier=1).then_inc(ident_ready, 1)
            pool.wait_ge(ident_ready, 1)
            pool.tensor_copy(identb[:], ident[:]).then_inc(consts, 2)
            pool.affine_select(out=mask_q[:], in_=mask_q[:], compare_op=ALU.is_ge, fill=MASKED, base=0,
                               pattern=[[-1, P]], channel_multiplier=1).then_inc(consts, 1)
            pool.affine_select(out=mask_k[:], in_=mask_k[:], compare_op=ALU.is_ge, fill=MASKED, base=0,
                               pattern=[[1, P]], channel_multiplier=-1).then_inc(consts, 1)

            def split_x(n):
                if not (isinstance(n, int) and n == 0):
                    await_parts(pool, pool_passed, n - 1, GROUPS - 2)
                plain(pool, x_in, 16 * (n + 1), pool_passed)
                for c in range(DC):
                    ins = pool.tensor_copy(xs[:, HI, c, :], nat[:, c, :])
                ins.then_inc(x_split, 1)
                pool.wait_ge(x_split, 2 * n + 1)
                for c in range(DC):
                    ins = pool.tensor_tensor(xs[:, LO, c, :], nat[:, c, :], raw(xs[:, HI, c, :]), ALU.subtract)
                ins.then_inc(x_split, 1)

            def run(b):
                if not (isinstance(b, int) and b == NB - 1):
                    split_x(b + 1)
                for t in range(TT):
                    pool.wait_ge(res_in[t % 2], 16 * (b * (TT // 2) + t // 2 + 1))
                    pool.tensor_tensor(xres[:, t % 2], xres[:, t % 2], keep["bo"][:], ALU.add).then_inc(bo_added, 1)

            split_x(0)
            each_batch(pool, run)

        @block.tensor
        def _(pe):
            def take(bank, turn, off):
                pe.wait_ge(bank_free[bank], off + turn)

            def run(b, lead=False):
                order, at, off = scope(b, lead)
                nxt = 0 if lead else b * GROUPS + 1
                for item in order:
                    kind = item[0]
                    if kind == "scores":
                        scores(b, *item[1:])
                        continue
                    if kind == "values":
                        values(b, *item[1:])
                        continue
                    if kind == "sums":
                        weigh(item[2], db, lambda h, j: ones[:]).then_inc(pv_done, 1)
                        continue
                    bank, turn = at[item]
                    out = shared[:, bank, :]
                    if kind == "maxT":
                        pe.wait_ge(mx_joined, 2 if lead else 2 * (nxt + item[1] + 1))
                    take(bank, turn, off)
                    if kind == "v":
                        t = item[1]
                        if t == 0:
                            pe.wait_ge(x_split, 2 * (b + 1))
                        mm = product(out, [(xs[:, a, c, t * P:(t + 1) * P], keep["wv"][:, w, c, :])
                                           for a, w in ((HI, HI), (LO, HI), (HI, LO)) for c in range(DC)])
                        mm.then_inc(bank_full[bank], 1)
                    elif kind == "proj":
                        g, i = item[1], item[2]
                        if i == 0:
                            pe.wait_ge(w_in, 16 * (1 if lead else nxt + g + 1))
                            if lead:
                                pe.wait_ge(x_split, 2)
                            elif g == GROUPS - 1:
                                pe.wait_ge(x_split, 2 * (b + 2))
                        which, hh = i // 2, i % 2
                        mm = product(out, [(wqk[:, 2 * which + w, c, :], xs[:, a, c, hh * HALF:(hh + 1) * HALF])
                                           for a, w in ((HI, HI), (LO, HI), (HI, LO)) for c in range(DC)])
                        mm.then_inc(bank_full[bank], 1)
                    elif kind == "max":
                        g, (h, _, it, k0, n) = item[1], maxes[item[2]]
                        if item[2] % 12 == 0:
                            pe.wait_ge(strips_sent[h], (1 if lead else nxt + g + 1) * STRIPS)
                        buf = (g + 1) % 2
                        diag = k0 + n == (it + 1) * P
                        mm = pe.matmul(out[:, 0:n], q_ops[0:MAX_STRIP, buf, h, it * P:(it + 1) * P],
                                       k_ops[0:MAX_STRIP, buf, h, k0:k0 + n], start=True, stop=not diag)
                        if diag:
                            mm = pe.matmul(out[:, n - P:n], identb[:], mask_q[:], start=False, stop=True)
                        mm.then_inc(bank_full[bank], 1)
                    elif kind == "maxT":
                        pe.transpose(out[0:HG * TT, 0:P], mrow[:].rearrange("p h t -> p (h t)"), ident[:]
                                     ).then_inc(bank_full[bank], 1)
                    elif kind == "out":
                        t = item[1]
                        if t == 0:
                            pe.wait_ge(normed, 2 * GROUPS * (b + 1))
                        mm = product(out, [(y[:, c, t * P:(t + 1) * P], keep["wo"][:, c, :]) for c in range(DC)])
                        mm.then_inc(bank_full[bank], 1)

            def product(out, pairs):
                for n, (a, c) in enumerate(pairs):
                    mm = pe.matmul(out, a, c, start=(n == 0), stop=(n == len(pairs) - 1))
                return mm

            def scores(b, g, k, pair):
                hh, j, c0 = steps[k]
                buf = g % 2
                s = (b * GROUPS + g) * NE + k
                if k == 0 and pair == 0:
                    pe.wait_ge(m_sent, 32 * (b * GROUPS + g + 1))
                pe.wait_ge(exp_done, 2 * s + pair + 1)
                for q in range(2):
                    h = 2 * pair + q
                    out = st[:, pair, q, :]
                    diag = j * P >= hh * HALF
                    mm = pe.matmul(out[:, c0:HALF], k_ops[:, buf, h, j * P:(j + 1) * P],
                                   q_ops[:, buf, h, hh * HALF + c0:(hh + 1) * HALF], start=True, stop=not diag)
                    if diag:
                        mm = pe.matmul(out[:, c0:c0 + P], identb[:], mask_k[:], start=False, stop=True)
                mm.then_inc(st_full, 1)

            def values(b, g, k):
                hh, j, c0 = steps[k]
                s = (b * GROUPS + g) * NE + k
                if g == 0 and k == 0:
                    _, at, off = scope(b)
                    for t in (TT - 2, TT - 1):
                        bank, turn = at[("v", t)]
                        pe.wait_ge(bank_free[bank], off + turn + 1)
                if j == 0:
                    pe.wait_ge(normed, 2 * (b * GROUPS + g) + hh)
                pe.wait_ge(exp_done, 2 * s + 4)
                weigh(k, yb, lambda h, j: v[:, j, g * P + h * DH:g * P + (h + 1) * DH])

            def weigh(k, bank, rows):
                hh, j, c0 = steps[k]
                for h in range(HG):
                    mm = pe.matmul(bank[h * DH:(h + 1) * DH, c0:HALF], rows(h, j),
                                   probs[:, slot_of(k, h // 2), h % 2, c0:HALF],
                                   start=(j == 0), stop=(j == 4 * hh + 3), tile_position=(0, h * DH))
                return mm

            pe.wait_ge(consts, N_CONSTS)
            run(0, lead=True)
            each_batch(pe, run)

        @block.scalar
        def _(act):
            def run(b, lead=False):
                order, at, off = scope(b, lead)
                for item in order:
                    kind = item[0]
                    if kind == "scores":
                        exps(b, *item[1:])
                        continue
                    if not uses_bank(item):
                        continue
                    bank, turn = at[item]
                    src = shared[:, bank, :]
                    if kind == "v":
                        act.wait_ge(bank_full[bank], off + turn + 1)
                        act.activation(v[:, item[1], :], src, ACT.Copy).then_inc(bank_free[bank], 1)
                    elif kind == "proj":
                        g, i = item[1], item[2]
                        which, hh = i // 2, i % 2
                        act.wait_ge(bank_full[bank], off + turn + 1)
                        if i == 0:
                            if lead:
                                act.wait_ge(x_split, 2)
                            elif g == GROUPS - 1:
                                act.wait_ge(x_split, 2 * (b + 2))
                            if not lead:
                                for h in range(HG):
                                    act.wait_ge(strips_sent[h], (b * GROUPS + g + 1) * STRIPS)
                        gn = (g + 1) % GROUPS
                        bias = (keep["bq"], keep["bk"])[which]
                        act.activation(nat[:, 2 * which + HI, hh * HALF:(hh + 1) * HALF].bitcast(F32R), src,
                                       ACT.Identity, bias=bias[:, gn:gn + 1]).then_inc(hi_ready, 1)
                    elif kind == "maxT":
                        act.wait_ge(bank_full[bank], off + turn + 1)
                        n = 0 if lead else b * GROUPS + item[1] + 1
                        act.wait_ge(m_sent, 32 * n)
                        act.activation(mneg[:, HI, :], src[0:HG * TT, 0:P], ACT.Copy, scale=-1.0).then_inc(mneg_hi, 1)
                        act.wait_ge(bank_free[bank], off + turn + 1)
                        dst = q_ops[:, (item[1] + 1) % 2]
                        for part in (HI, LO):
                            act.dma_start(raw(dst[MAX_STRIP + part:MAX_STRIP + part + 1, :, :]).rearrange(
                                "a h (t p) -> a (h t) p", p=P), raw(mneg[:, part, :])).then_inc(m_sent, 16)
                    elif kind == "out":
                        t = item[1]
                        act.wait_ge(mv_ready, b * TT + t + 1)
                        act.activation(std[:, t % 2:t % 2 + 1], mv[:, t % 2, 1:2], ACT.Sqrt, bias=eps[:]
                                       ).then_inc(std_ready, 1)

            def exps(b, g, k, pair):
                c0 = steps[k][2]
                s = (b * GROUPS + g) * NE + k
                act.wait_ge(st_full, 2 * s + pair + 1)
                if pair == 0:
                    act.wait_ge(pv_done, s)
                act.activation(probs[:, slot_of(k, pair), :, c0:HALF], st[:, pair, :, c0:HALF], ACT.Exp,
                               scale=SCALE).then_inc(exp_done, 1)

            act.wait_ge(consts, N_CONSTS)
            act.activation(std[:, 0:1], eps[:], ACT.Copy).then_inc(exp_done, 2)
            run(0, lead=True)
            each_batch(act, run)

        @block.vector
        def _(dve):
            def run(b, lead=False):
                order, at, off = scope(b, lead)
                for item in order:
                    kind = item[0]
                    if kind == "sums" and steps[item[2]][1] == 4 * steps[item[2]][0] + 3:
                        normalise(b, item[1], steps[item[2]][0], item[2])
                    if not uses_bank(item):
                        continue
                    bank, turn = at[item]
                    src = shared[:, bank, :]
                    if kind == "proj":
                        g, i = item[1], item[2]
                        which, hh = i // 2, i % 2
                        n = 4 * (0 if lead else b * GROUPS + g + 1) + i
                        dve.wait_ge(hi_ready, n + 1)
                        gn = (g + 1) % GROUPS
                        bias = (keep["bq"], keep["bk"])[which]
                        cols = slice(hh * HALF, (hh + 1) * HALF)
                        dve.scalar_tensor_tensor(out=nat[:, 2 * which + LO, cols].bitcast(F32R), in0=src,
                                                 scalar=bias[:, gn:gn + 1], in1=nat[:, 2 * which + HI, cols],
                                                 op0=ALU.add, op1=ALU.subtract
                                                 ).then_inc(bank_free[bank], 1)
                    elif kind == "max":
                        h, slot, it, k0, n = maxes[item[2]]
                        dve.wait_ge(bank_full[bank], off + turn + 1)
                        dve.tensor_reduce(mx[:, h, slot:slot + 1], src[:, 0:n], AX.X, ALU.max
                                          ).then_inc(bank_free[bank], 1)
                    elif kind == "maxT":
                        n = 0 if lead else b * GROUPS + item[1] + 1
                        for k in range(2):
                            dve.wait_ge(bank_free[k], off + (turn if k == bank else turn_of_other(at[item])))
                        dve.tensor_copy(mrow[:, :, 0:4], mx[:, :, 0:4]).then_inc(mx_joined, 1)
                        dve.tensor_tensor(mrow[:, :, 4:8], mx[:, :, 4:8], mx[:, :, 8:12], ALU.max
                                          ).then_inc(mx_joined, 1)
                        dve.wait_ge(mneg_hi, n + 1)
                        dve.scalar_tensor_tensor(out=mneg[:, LO, :], in0=src[0:HG * TT, 0:P], scalar=-1.0,
                                                 in1=raw(mneg[:, HI, :]), op0=ALU.mult, op1=ALU.subtract
                                                 ).then_inc(bank_free[bank], 1)
                    elif kind == "out":
                        layer_norm(b, item[1], bank, off + turn, src)

            def turn_of_other(bank_turn):
                bank, turn = bank_turn
                return turn if bank == 0 else turn + 1

            def normalise(b, g, hh, k):
                n = 2 * (b * GROUPS + g) + hh
                dve.wait_ge(pv_done, (b * GROUPS + g) * NE + k + 2)
                dve.reciprocal(rden[:], db[:]).then_inc(rden_ready, 1)
                dve.wait_ge(rden_ready, n + 1)
                dve.tensor_tensor(y[:, g, hh * HALF:(hh + 1) * HALF], yb[:], rden[:], ALU.mult).then_inc(normed, 1)

            def layer_norm(b, t, bank, turn, src):
                n = b * TT + t
                r = t % 2
                dve.wait_ge(bank_full[bank], turn + 1)
                dve.wait_ge(bo_added, n + 1)
                dve.wait_ge(x1_out[r], 16 * (b * (TT // 2) + t // 2))
                dve.tensor_tensor(x1[:, r], src, xres[:, r], ALU.add).then_inc(summed, 1)
                dve.wait_ge(summed, n + 1)
                dve.bn_stats(stats[:, t, :], x1[:, r]).then_inc(bank_free[bank], 1)
                plain(dve, bank_free[bank], turn + 1, dve_passed)
                dve.bn_aggr(mv[:, r, :], stats[:, t, :]).then_inc(mv_ready, 1)
                dve.wait_ge(std_ready, n + 1)
                dve.reciprocal(rstd[:, r:r + 1], std[:, r:r + 1]).then_inc(rstd_ready, 1)
                dve.wait_ge(rstd_ready, n + 1)
                dve.tensor_scalar(x1[:, r], x1[:, r], mv[:, r, 0:1], rstd[:, r:r + 1], ALU.subtract, ALU.mult
                                  ).then_inc(x1_ready, 1)

            dve.memset(raw(q_ops[MAX_STRIP:P]), 0.0).then_inc(consts, 1)
            dve.memset(raw(k_ops[MAX_STRIP:P]), 0.0).then_inc(strip_zero, 1)
            dve.wait_ge(strip_zero, 1)
            dve.memset(raw(k_ops[MAX_STRIP:MAX_STRIP + 2]), 1.0).then_inc(consts, 1)
            dve.memset(rden[:], 0.0).then_inc(pv_done, 1)
            run(0, lead=True)
            each_batch(dve, run)


E_N = 16
F_N = 2048
FC = F_N // P
TABLE = D + E_N
ACC = D + 4
QT = HALF // P
BLK = 4
NBLK = FC // BLK


def build_router(nc, x1_dram, w, table, logits_dram, acc_dram, logits, NB):
    with ExitStack() as ctx:
        sb = lambda name, shape, dt=F32: ctx.enter_context(nc.sbuf_tensor(name, shape, dt))
        ps = lambda name, shape, dt=F32: ctx.enter_context(nc.psum_tensor(name, shape, dt))
        sem = lambda name: ctx.enter_context(nc.semaphore(name))
        x1 = sb("r_x1", [P, 2, QT, D])
        xn = sb("r_xn", [P, 2, QT, D])
        xnT = sb("r_xnT", [P, 2, DC, HALF])
        square = sb("r_square", [P, 2, D])
        ss = sb("r_ss", [P, 2, QT])
        rms = sb("r_rms", [P, 2, QT])
        rinv = sb("r_rinv", [P, 2, QT])
        nw = sb("r_norm_weight", [P, D])
        rw = sb("r_weight", [P, DC, E_N])
        rb = sb("r_bias", [E_N, 1])
        eps = sb("r_eps", [P, 1])
        ident = sb("r_ident", [P, P])
        zeros = sb("r_zeros", [P, QT, ACC])
        ps_t = ps("r_ps_t", [P, DC, HALF])
        ps_l = ps("r_ps_l", [E_N, 2, HALF])
        w_in, zeroed, cleared, consts = sem("r_w_in"), sem("r_zeroed"), sem("r_cleared"), sem("r_consts")
        x_in = [sem(f"r_x_in{u}") for u in range(2)]
        xn_out = [sem(f"r_xn_out{u}") for u in range(2)]
        ss_ready, rms_ready, rinv_ready, xn_ready = sem("ss_ready"), sem("rms_ready"), sem("rinv_ready"), sem("xn_ready")
        t_full = sem("t_full")
        act_copied, dve_copied = sem("act_copied"), sem("dve_copied")
        l_full, l_copied, l_out = sem("l_full"), sem("l_copied"), sem("l_out")
        block = ctx.enter_context(nc.Block())
        tokens = lambda dram, it, u: dram[bass.ds(it * T + u * HALF, HALF), :].rearrange("(t p) d -> p t d", p=P)

        @block.sync
        def _(sp):
            sp.dma_start(nw[:], w["norm"].rearrange("(a n) -> a n", a=1).to_broadcast([P, D])).then_inc(w_in, 16)
            with nc.allow_non_contiguous_dma(reason="small router bias"):
                sp.dma_start(rb[:], w["rb"].rearrange("(e a) -> e a", a=1)).then_inc(w_in, 16)
            sp.dma_start(rw[:], w["rwT"].rearrange("(c p) e -> p c e", p=P)).then_inc(w_in, 16)
            sp.wait_ge(zeroed, 1)
            with sp.Fori(0, NB) as it:
                for u in range(2):
                    sp.wait_ge(xn_ready, 2 * it + max(u - 1, 0))
                    sp.dma_start(x1[:, u], tokens(x1_dram, it, u)).then_inc(x_in[u], 16)
                    sp.dma_start(acc_dram[bass.ds(it * T + u * HALF, HALF), :].rearrange("(t p) d -> p t d", p=P),
                                 zeros[:]).then_inc(cleared, 16)
                for u in range(2):
                    sp.wait_ge(xn_ready, 2 * it + u + 1)
                    sp.dma_start(tokens(table, it, u)[:, :, 0:D], xn[:, u]).then_inc(xn_out[u], 16)
                sp.wait_ge(l_copied, 2 * it + 2)
                sp.dma_start(logits_dram[:, bass.ds(it * T, T)], logits[:, bass.ds(it * T, T)]).then_inc(l_out, 16)
            sp.wait_ge(l_out, 16 * NB)
            sp.wait_ge(cleared, 32 * NB)
            for u in range(2):
                sp.wait_ge(xn_out[u], 16 * NB)

        @block.gpsimd
        def _(pool):
            pool.memset(zeros[:], 0.0).then_inc(zeroed, 1)
            pool.memset(eps[:], EPS).then_inc(consts, 1)
            pool.memset(ident[:], 0.0).then_inc(zeroed, 1)
            pool.wait_ge(zeroed, 2)
            pool.affine_select(out=ident[:], in_=ident[:], compare_op=ALU.not_equal, fill=1.0, base=0,
                               pattern=[[-1, P]], channel_multiplier=1).then_inc(consts, 1)

        @block.scalar
        def _(act):
            act.wait_ge(consts, 2)
            with act.Fori(0, NB) as it:
                for u in range(2):
                    n = 2 * it + u
                    act.wait_ge(x_in[u], 16 * (it + 1))
                    act.wait_ge(rinv_ready, n)
                    for t in range(QT):
                        act.activation(square[:, t % 2], x1[:, u, t, :], ACT.Square, accum_out=ss[:, u, t:t + 1]
                                       ).then_inc(ss_ready, 1)
                        act.wait_ge(ss_ready, QT * n + t + 1)
                    act.activation(rms[:, u], ss[:, u], ACT.Sqrt, bias=eps[:], scale=1.0 / D).then_inc(rms_ready, 1)
                    for c in range(0, DC, 2):
                        act.wait_ge(t_full, DC * n + c + 1)
                        act.wait_ge(l_full, 2 * it)
                        act.activation(xnT[:, u, c, :], ps_t[:, c, :], ACT.Copy).then_inc(act_copied, 1)

        @block.vector
        def _(dve):
            dve.wait_ge(w_in, 48)
            with dve.Fori(0, NB) as it:
                for u in range(2):
                    n = 2 * it + u
                    dve.wait_ge(rms_ready, n + 1)
                    dve.reciprocal(rinv[:, u], rms[:, u]).then_inc(rinv_ready, 1)
                    dve.wait_ge(rinv_ready, n + 1)
                    dve.wait_ge(xn_out[u], 16 * it)
                    dve.wait_ge(t_full, DC * 2 * it)
                    for t in range(QT):
                        ins = dve.scalar_tensor_tensor(out=xn[:, u, t, :], in0=x1[:, u, t, :],
                                                       scalar=rinv[:, u, t:t + 1], in1=nw[:],
                                                       op0=ALU.mult, op1=ALU.mult)
                    ins.then_inc(xn_ready, 1)
                    for c in range(1, DC, 2):
                        dve.wait_ge(t_full, DC * n + c + 1)
                        dve.wait_ge(l_full, 2 * it)
                        dve.tensor_copy(xnT[:, u, c, :], ps_t[:, c, :]).then_inc(dve_copied, 1)
                    dve.wait_ge(l_full, n + 1)
                    dve.tensor_scalar(logits[:, bass.ds(n * HALF, HALF)], ps_l[:, u, :], rb[:, 0:1], None, ALU.add
                                      ).then_inc(l_copied, 1)

        @block.tensor
        def _(pe):
            pe.wait_ge(consts, 2)
            pe.wait_ge(w_in, 48)
            with pe.Fori(0, NB) as it:
                for u in range(2):
                    n = 2 * it + u
                    pe.wait_ge(xn_ready, n + 1)
                    pe.wait_ge(act_copied, 2 * n)
                    pe.wait_ge(dve_copied, 2 * n)
                    for c in range(DC):
                        for t in range(QT):
                            mm = pe.transpose(ps_t[:, c, t * P:(t + 1) * P], xn[:, u, t, c * P:(c + 1) * P], ident[:])
                        mm.then_inc(t_full, 1)
                    pe.wait_ge(l_copied, 2 * it)
                    pe.wait_ge(act_copied, 2 * n + 2)
                    pe.wait_ge(dve_copied, 2 * n + 2)
                    for c in range(DC):
                        mm = pe.matmul(ps_l[:, u, :], rw[:, c, :], xnT[:, u, c, :], start=(c == 0), stop=(c == DC - 1))
                    mm.then_inc(l_full, 1)


def build_selection(nc, table, logits_dram, list_dram, logits, NB):
    N = NB * T
    CAP = N // E_N
    ROWS = E_N * NB
    NCH = N // P
    LO_N = 32
    HI_N = max(CAP // LO_N, 1)
    with ExitStack() as ctx:
        sb = lambda name, shape, dt=F32: ctx.enter_context(nc.sbuf_tensor(name, shape, dt))
        ps = lambda name, shape, dt=F32: ctx.enter_context(nc.psum_tensor(name, shape, dt))
        sem = lambda name: ctx.enter_context(nc.semaphore(name))
        ident = sb("s_ident", [P, P])
        same = sb("s_same_expert", [ROWS, E_N, NB])
        before = sb("s_earlier_sequence", [ROWS, E_N, NB])
        lg = sb("s_logits_tokens", [P, NCH, E_N])
        red = sb("s_red", [P, 3, NCH])
        x = sb("s_x", [ROWS, T])
        xs = sb("s_x_signed", [ROWS, T])
        junk = sb("s_junk", [ROWS, T])
        gt = sb("s_above", [ROWS, T])
        eq = sb("s_equal", [ROWS, T])
        ones = sb("s_ones", [ROWS, T])
        scan = sb("s_scan", [ROWS, T])
        sel = sb("s_selected", [ROWS, T])
        pos = sb("s_place", [ROWS, T])
        small = sb("s_small", [ROWS, 16])
        bit = sb("s_bit", [ROWS, 1], I32)
        thr = sb("s_threshold", [ROWS, 1], I32)
        cand = sb("s_candidate", [ROWS, 1], I32)
        keep = sb("s_keep", [ROWS, 1], U32)
        place = sb("s_place_tokens", [P, TT, E_N, NB], I32)
        row = sb("s_list_row", [P, TT, E_N, NB], I32)
        col = sb("s_list_col", [P, TT, E_N, NB], I32)
        iota_i = sb("s_iota_i", [P, LO_N], I32)
        iota = sb("s_iota", [P, LO_N], F32)
        cid_i = sb("s_chunk_i", [P, TT, NB], I32)
        cid = sb("s_chunk", [P, TT, NB], BF16)
        pid_i = sb("s_partition_i", [P, 1], I32)
        pid = sb("s_partition", [P, 1])
        oh_row = sb("s_row_onehot", [P, 2, TT, NB, HI_N], BF16)
        oh_col = sb("s_col_onehot", [P, 2, TT, NB, LO_N], BF16)
        oh_tok = sb("s_col_tokens", [P, 2, TT, NB, 2, LO_N], BF16)
        parts = sb("s_list_parts", [HI_N, 2, 2, LO_N])
        lists = sb("s_list", [HI_N, 2, LO_N], U32)
        ps_lg = ps("s_ps_lg", [P, NCH, E_N])
        ps_pos = ps("s_ps_pos", [P, TT, ROWS])
        ps_cnt = ps("s_ps_cnt", [ROWS, 16])
        ps_list = ps("s_ps_list", [HI_N, 2, HALF])
        consts, made, x_in, lg_full = sem("s_consts"), sem("s_made"), sem("s_x_in"), sem("s_lg_full")
        d = sem("s_dve_step")
        shifted, exped, probs_ready, probs_out = sem("s_shifted"), sem("s_exped"), sem("s_probs_ready"), sem("s_probs_out")
        passed = sem("s_passed")
        counted, grouped = sem("s_counted"), sem("s_grouped")
        tallied, offset = sem("s_tallied"), sem("s_offset")
        pos_ready, pos_turned, places, onehots, list_mm, list_ready, list_copied = (
            sem("s_pos_ready"), sem("s_pos_turned"), sem("s_places"), sem("s_onehots"), sem("s_list_mm"),
            sem("s_list_ready"), sem("s_list_copied"))
        list_out = [sem(f"s_list_out{r}") for r in range(2)]
        block = ctx.enter_context(nc.Block())
        BITS = 31

        @block.sync
        def _(sp):
            sp.dma_start(x[:], logits_dram.rearrange("e (s t) -> (e s) t", t=T)).then_inc(x_in, 16)
            sp.wait_ge(probs_ready, 1)
            sp.dma_start(table.rearrange("(c p) k -> p c k", p=P)[:, :, D:TABLE], lg[:]).then_inc(probs_out, 16)
            with sp.Fori(0, E_N // 2) as it:
                for r in range(2):
                    e = 2 * it + r
                    sp.wait_ge(list_ready, e + 1)
                    sp.dma_start(list_dram[bass.ds(e, 1), :].rearrange("a (h l) -> (a h) l", l=LO_N), lists[:, r, :]
                                 ).then_inc(list_out[r], 16)
            sp.wait_ge(probs_out, 16)
            for r in range(2):
                sp.wait_ge(list_out[r], 16 * E_N // 2)

        @block.gpsimd
        def _(pool):
            pool.memset(ident[:], 0.0).then_inc(made, 1)
            pool.memset(same[:], 1.0).then_inc(made, 1)
            pool.iota(iota_i[:], pattern=[[1, LO_N]], base=0, channel_multiplier=0).then_inc(made, 1)
            pool.iota(cid_i[:], pattern=[[1, TT], [TT, NB]], base=0, channel_multiplier=0).then_inc(made, 1)
            pool.iota(pid_i[:], pattern=[[0, 1]], base=0, channel_multiplier=1).then_inc(made, 1)
            pool.wait_ge(made, 5)
            pool.affine_select(out=ident[:], in_=ident[:], compare_op=ALU.not_equal, fill=1.0, base=0,
                               pattern=[[-1, P]], channel_multiplier=1).then_inc(consts, 1)
            pool.affine_select(out=same[:], in_=same[:], compare_op=ALU.is_ge, fill=0.0, base=0,
                               pattern=[[-NB, E_N], [0, NB]], channel_multiplier=1).then_inc(made, 1)
            pool.wait_ge(made, 6)
            pool.affine_select(out=same[:], in_=same[:], compare_op=ALU.is_ge, fill=0.0, base=NB - 1,
                               pattern=[[NB, E_N], [0, NB]], channel_multiplier=-1).then_inc(made, 1)
            pool.wait_ge(made, 7)
            pool.affine_select(out=before[:], in_=same[:], compare_op=ALU.is_gt, fill=0.0, base=0,
                               pattern=[[NB, E_N], [1, NB]], channel_multiplier=-1).then_inc(consts, 1)

        @block.scalar
        def _(act):
            act.wait_ge(shifted, 1)
            act.activation(lg[:], lg[:], ACT.Exp).then_inc(exped, 1)

        @block.tensor
        def _(pe):
            pe.wait_ge(consts, 2)
            for c in range(NCH):
                mm = pe.transpose(ps_lg[:, c, :], logits[:, c * P:(c + 1) * P], ident[0:E_N, 0:E_N])
            mm.then_inc(lg_full, 1)
            group = same[:].rearrange("k e s -> k (e s)")
            pe.wait_ge(counted, 1)
            pe.matmul(ps_cnt[:, 0:1], group, small[:, 0:1], start=True, stop=True).then_inc(grouped, 1)
            with pe.Fori(0, BITS) as i:
                pe.wait_ge(counted, i + 2)
                pe.matmul(ps_cnt[:, 1:2], group, small[:, 4:5], start=True, stop=True).then_inc(grouped, 1)
            pe.wait_ge(tallied, 1)
            pe.matmul(ps_cnt[:, 2:3], group, small[:, 5:6], start=True, stop=True)
            pe.matmul(ps_cnt[:, 3:4], before[:].rearrange("k e s -> k (e s)"), scan[:, T - 1:T], start=True, stop=True
                      ).then_inc(offset, 1)
            pe.wait_ge(tallied, 2)
            pe.matmul(ps_cnt[:, 4:5], before[:].rearrange("k e s -> k (e s)"), scan[:, T - 1:T], start=True, stop=True
                      ).then_inc(offset, 1)
            pe.wait_ge(pos_ready, 1)
            for b in range(TT):
                mm = pe.transpose(ps_pos[:, b, :], pos[:, b * P:(b + 1) * P], ident[0:ROWS, 0:ROWS])
            mm.then_inc(pos_turned, 1)
            with pe.Fori(0, E_N // 2) as it:
                for r in range(2):
                    e = 2 * it + r
                    pe.wait_ge(onehots, e + 1)
                    pe.wait_ge(list_copied, 2 * it)
                    for n in range(NCH):
                        b, s = n // NB, n % NB
                        mm = pe.matmul(ps_list[:, r, 0:2 * LO_N], oh_row[:, r, b, s, :],
                                       oh_tok[:, r, b, s].rearrange("p a l -> p (a l)"),
                                       start=(n == 0), stop=(n == NCH - 1))
                    mm.then_inc(list_mm, 1)

        @block.vector
        def _(dve):
            step = [0]

            def then(ins):
                step[0] += 1
                ins.then_inc(d, 1)
                dve.wait_ge(d, step[0])

            dve.wait_ge(lg_full, 1)
            then(dve.tensor_reduce(red[:, 0, :], ps_lg[:], AX.X, ALU.max))
            dve.tensor_tensor(lg[:], ps_lg[:], red[:, 0, :].unsqueeze(2).to_broadcast([P, NCH, E_N]), ALU.subtract
                              ).then_inc(shifted, 1)
            dve.wait_ge(x_in, 16)
            then(dve.tensor_scalar(junk[:], x[:], 0.0, None, ALU.is_ge, ALU.add, accum_out=small[:, 0:1]))
            dve.memset(ones[:], 1.0).then_inc(counted, 1)
            dve.wait_ge(exped, 1)
            then(dve.tensor_reduce(red[:, 1, :], lg[:], AX.X, ALU.add))
            then(dve.reciprocal(red[:, 2, :], red[:, 1, :]))
            dve.tensor_tensor(lg[:], lg[:], red[:, 2, :].unsqueeze(2).to_broadcast([P, NCH, E_N]), ALU.mult
                              ).then_inc(probs_ready, 1)
            dve.wait_ge(grouped, 1)
            then(dve.tensor_scalar(small[:, 1:2], ps_cnt[:, 0:1], float(CAP), None, ALU.is_ge))
            then(dve.tensor_scalar(small[:, 2:3], small[:, 1:2], 2.0, -1.0, ALU.mult, ALU.add))
            then(dve.tensor_scalar(small[:, 3:4], small[:, 1:2], float(2 * CAP - N - 1), float(N - CAP + 1),
                                   ALU.mult, ALU.add))
            then(dve.tensor_scalar(xs[:], x[:], small[:, 2:3], None, ALU.mult))
            then(dve.memset(thr[:], 0))
            then(dve.memset(bit[:], 1 << (BITS - 1)))
            first = step[0]
            PER = 5
            with dve.Fori(0, BITS) as i:
                done = i * PER + first
                dve.tensor_tensor(cand[:], thr[:], bit[:], ALU.bitwise_or).then_inc(d, 1)
                dve.wait_ge(d, done + 1)
                dve.tensor_scalar(junk[:], xs[:], cand[:].bitcast(F32), None, ALU.is_ge, ALU.add,
                                  accum_out=small[:, 4:5]).then_inc(counted, 1)
                dve.tensor_scalar(bit[:], bit[:], 1, None, ALU.logical_shift_right).then_inc(d, 1)
                dve.wait_ge(grouped, i + 2)
                dve.wait_ge(d, done + 2)
                dve.tensor_tensor(small[:, 6:7], ps_cnt[:, 1:2], small[:, 3:4], ALU.is_ge).then_inc(d, 1)
                dve.wait_ge(d, done + 3)
                dve.tensor_copy(keep[:], small[:, 6:7]).then_inc(d, 1)
                plain(dve, d, done + 4, passed)
                dve.copy_predicated(thr[:], keep[:], cand[:]).then_inc(d, 1)
                dve.wait_ge(d, done + 5)
            step[0] = first + BITS * PER
            then(dve.tensor_scalar(small[:, 7:8], thr[:].bitcast(F32), small[:, 2:3], None, ALU.mult))
            then(dve.tensor_scalar(gt[:], x[:], small[:, 7:8], None, ALU.is_gt, ALU.add, accum_out=small[:, 5:6]))
            then(dve.tensor_scalar(eq[:], x[:], small[:, 7:8], None, ALU.is_equal))
            dve.tensor_tensor_scan(scan[:], ones[:], eq[:], 0.0, ALU.mult, ALU.add).then_inc(tallied, 1)
            dve.wait_ge(offset, 1)
            then(dve.tensor_scalar(small[:, 8:9], ps_cnt[:, 2:3], -1.0, float(CAP), ALU.mult, ALU.add))
            then(dve.tensor_tensor(small[:, 9:10], small[:, 8:9], ps_cnt[:, 3:4], ALU.subtract))
            then(dve.scalar_tensor_tensor(out=sel[:], in0=scan[:], scalar=small[:, 9:10], in1=eq[:],
                                          op0=ALU.is_le, op1=ALU.mult))
            then(dve.tensor_tensor(sel[:], sel[:], gt[:], ALU.add))
            dve.tensor_tensor_scan(scan[:], ones[:], sel[:], 0.0, ALU.mult, ALU.add).then_inc(tallied, 1)
            dve.wait_ge(offset, 2)
            then(dve.tensor_copy(small[:, 10:11], ps_cnt[:, 4:5]))
            dve.scalar_tensor_tensor(out=pos[:], in0=scan[:], scalar=small[:, 10:11], in1=sel[:],
                                     op0=ALU.add, op1=ALU.mult).then_inc(pos_ready, 1)
            then(dve.tensor_copy(iota[:], iota_i[:]))
            then(dve.tensor_copy(cid[:], cid_i[:]))
            then(dve.tensor_copy(pid[:], pid_i[:]))
            dve.wait_ge(pos_turned, 1)
            then(dve.tensor_scalar(place[:].rearrange("p b e s -> p b (e s)"), ps_pos[:], -1.0, None, ALU.add))
            then(dve.tensor_scalar(row[:], place[:], 5, None, ALU.arith_shift_right))
            then(dve.tensor_scalar(col[:], place[:], LO_N - 1, None, ALU.bitwise_and))
            first = step[0]
            PER2 = 2 + TT * 2
            with dve.Fori(0, E_N // 2) as it:
                for r in range(2):
                    e = 2 * it + r
                    dve.wait_ge(list_mm, 2 * it)
                    dve.tensor_tensor(
                        oh_row[:, r], row[:, :, bass.ds(e, 1), :].rearrange("p b a s -> p b (a s)").unsqueeze(3)
                        .to_broadcast([P, TT, NB, HI_N]),
                        iota[:, 0:HI_N].unsqueeze(1).unsqueeze(1).to_broadcast([P, TT, NB, HI_N]), ALU.is_equal)
                    dve.tensor_tensor(
                        oh_col[:, r], col[:, :, bass.ds(e, 1), :].rearrange("p b a s -> p b (a s)").unsqueeze(3)
                        .to_broadcast([P, TT, NB, LO_N]),
                        iota[:].unsqueeze(1).unsqueeze(1).to_broadcast([P, TT, NB, LO_N]), ALU.is_equal
                    ).then_inc(places, 1)
                    dve.wait_ge(places, e + 1)
                    dve.tensor_scalar(oh_tok[:, r, :, :, 0, :], oh_col[:, r], pid[:, 0:1], None, ALU.mult)
                    dve.tensor_tensor(oh_tok[:, r, :, :, 1, :], oh_col[:, r],
                                      cid[:].unsqueeze(3).to_broadcast([P, TT, NB, LO_N]), ALU.mult
                                      ).then_inc(onehots, 1)
                    dve.wait_ge(list_mm, e + 1)
                    dve.tensor_copy(parts[:, r], ps_list[:, r, 0:2 * LO_N].rearrange("h (a l) -> h a l", a=2)
                                    ).then_inc(list_copied, 1)
                    dve.wait_ge(list_copied, e + 1)
                    dve.wait_ge(list_out[r], 16 * it)
                    dve.scalar_tensor_tensor(out=lists[:, r], in0=parts[:, r, 1], scalar=float(P),
                                             in1=parts[:, r, 0], op0=ALU.mult, op1=ALU.add).then_inc(list_ready, 1)


def build_experts(nc, w, table, list_dram, acc_dram, NB):
    N = NB * T
    CAP = N // E_N
    CT = CAP // P
    with ExitStack() as ctx:
        sb = lambda name, shape, dt=F32: ctx.enter_context(nc.sbuf_tensor(name, shape, dt))
        ps = lambda name, shape, dt=F32: ctx.enter_context(nc.psum_tensor(name, shape, dt))
        sem = lambda name: ctx.enter_context(nc.semaphore(name))
        idx = sb("m_idx", [P, 2, CT], U32)
        xg = sb("m_rows", [P, 2, CT, TABLE])
        xe = sb("m_tokens_t", [P, 2, 2, DC, CAP], F32R)
        w1 = sb("m_w1_raw", [P, 2, DC, BLK * P])
        w2 = sb("m_w2_raw", [P, 2, BLK, D])
        w1s = sb("m_w1_parts", [P, 2, 2, DC, BLK * P], F32R)
        w2s = sb("m_w2_parts", [P, 2, 2, BLK, D], F32R)
        h = sb("m_hidden", [P, 2, CAP])
        hs = sb("m_hidden_parts", [P, 2, 2, CAP], F32R)
        b1 = sb("m_b1", [P, 2, FC])
        b2 = sb("m_b2", [P, 2, D])
        gates = sb("m_gates", [P, 2, CT])
        out = sb("m_out", [P, CT, ACC])
        ident = sb("m_ident", [P, P])
        ps_t = ps("m_ps_t", [P, 2, HALF])
        ps_h = ps("m_ps_h", [P, 2, HALF])
        ps_y = ps("m_ps_y", [P, CT, HALF])

        idx_in = [sem(f"idx_in{r}") for r in range(2)]
        gathered = [sem(f"gathered{r}") for r in range(2)]
        w1_in = [sem(f"w1_in{r}") for r in range(2)]
        w2_in = [sem(f"w2_in{r}") for r in range(2)]
        b_in = [sem(f"b_in{r}") for r in range(2)]
        passed = sem("m_passed")
        w_hi, w_lo = sem("w_hi"), sem("w_lo")
        t_full, xe_hi, xe_lo, gate_ready = sem("m_t_full"), sem("xe_hi"), sem("xe_lo"), sem("gate_ready")
        h_full, gelu_done, h_hi, h_lo, fc2_done = sem("h_full"), sem("gelu_done"), sem("h_hi"), sem("h_lo"), sem("fc2_done")
        y_copied, out_ready, scattered, consts, zeroed = (sem("y_copied"), sem("out_ready"), sem("scattered"),
                                                          sem("m_consts"), sem("m_zeroed"))
        block = ctx.enter_context(nc.Block())

        def each_pair(eng, run):
            with eng.Fori(0, E_N // 2 - 1) as it:
                run(it, False)
            run(E_N // 2 - 1, True)

        def has_next(last, r):
            return not (last and r == 1)

        TURN_AT = {6: (0, 1), 9: (2, 3)}

        PIECES = 4

        @block.sync
        def _(sp):
            def load_block(e, e_slot_free, blk):
                q = blk % 2
                if e_slot_free is not None:
                    sp.wait_ge(w_lo, e_slot_free)
                sp.dma_start(w1[:, q], w["w1T"][bass.ds(e, 1)].rearrange("a (c p) f -> p (a c) f", p=P)
                             [:, :, blk * BLK * P:(blk + 1) * BLK * P]).then_inc(w1_in[q], 16)
                sp.dma_start(w2[:, q], w["w2T"][bass.ds(e, 1), blk * BLK * P:(blk + 1) * BLK * P, :].rearrange(
                    "a (f p) n -> p (a f) n", p=P)).then_inc(w2_in[q], 16)

            def load_small(e, r):
                sp.dma_start(idx[:, r, :], list_dram[bass.ds(e, 1), :].rearrange("a (p j) -> p (a j)", j=CT)
                             ).then_inc(idx_in[r], 16)
                sp.dma_start(b1[:, r, :], w["b1T"][bass.ds(e, 1)].rearrange("a p f -> p (a f)")).then_inc(b_in[r], 16)
                sp.dma_start(b2[:, r, :], w["b2"][bass.ds(e, 1), :].to_broadcast([P, D])).then_inc(b_in[r], 16)

            load_small(0, 0)
            load_block(0, None, 0)
            load_block(0, None, 1)

            def run(it, last):
                for r in range(2):
                    e = 2 * it + r
                    for blk in range(NBLK):
                        if blk == 1 and has_next(last, r):
                            sp.wait_ge(scattered, 16 * CT * e)
                            load_small(e + 1, 1 - r)
                        nb = blk + 2
                        if nb < NBLK:
                            load_block(e, PIECES * (e * NBLK + blk + 1), nb)
                        elif has_next(last, r):
                            load_block(e + 1, PIECES * (e * NBLK + blk + 1), nb - NBLK)

            each_pair(sp, run)

        @block.gpsimd
        def _(pool):
            pool.memset(out[:], 0.0).then_inc(consts, 1)
            pool.memset(ident[:], 0.0).then_inc(zeroed, 1)
            pool.wait_ge(zeroed, 1)
            pool.affine_select(out=ident[:], in_=ident[:], compare_op=ALU.not_equal, fill=1.0, base=0,
                               pattern=[[-1, P]], channel_multiplier=1).then_inc(consts, 1)

            def gather(e, r, count):
                plain(pool, idx_in[r], 16 * count, passed)
                for j in range(CT):
                    pool.indirect_dma_start(out=xg[:, r, j, :], out_offset=None, in_=table[:, :],
                                            in_offset=bass.IndirectOffsetOnAxis(ap=idx[:, r, j:j + 1], axis=0)
                                            ).then_inc(gathered[r], 16)

            def run(it, last):
                for r in range(2):
                    e = 2 * it + r
                    if has_next(last, r):
                        pool.wait_ge(xe_lo, DC * e + 1)
                        pool.wait_ge(gate_ready, e)
                        gather(e + 1, 1 - r, it + r + 1)
                    pool.wait_ge(scattered, 16 * CT * e)
                    for j in range(CT):
                        plain(pool, out_ready, CT * e + j + 1, passed)
                        pool.indirect_dma_start(out=acc_dram[:, :], out_offset=bass.IndirectOffsetOnAxis(
                            ap=idx[:, r, j:j + 1], axis=0), in_=out[:, j, :], in_offset=None,
                            compute_op=ALU.add).then_inc(scattered, 16)

            gather(0, 0, 1)
            each_pair(pool, run)
            pool.wait_ge(scattered, 16 * CT * E_N)

        @block.scalar
        def _(act):
            def split_hi(B, q, piece):
                n = 2 * (piece % 2)
                if piece < 2:
                    act.activation(w1s[:, q, HI, n:n + 2, :], w1[:, q, n:n + 2, :], ACT.Copy).then_inc(w_hi, 1)
                else:
                    act.activation(w2s[:, q, HI, n:n + 2, :], w2[:, q, n:n + 2, :], ACT.Copy).then_inc(w_hi, 1)

            def token_hi(r, c, cc):
                act.wait_ge(t_full, cc + 1)
                act.activation(xe[:, r, HI, c, :], ps_t[:, c % 2, 0:CAP], ACT.Copy).then_inc(xe_hi, 1)

            act.wait_ge(consts, 2)
            act.activation(gates[:, 0, :], ident[:, 0:CT], ACT.Copy).then_inc(gelu_done, 2)
            act.wait_ge(w1_in[0], 16)
            act.wait_ge(w2_in[0], 16)
            for piece in range(PIECES):
                split_hi(0, 0, piece)
            for c in range(DC):
                token_hi(0, c, c)

            def run(it, last):
                for r in range(2):
                    e = 2 * it + r
                    act.wait_ge(b_in[r], 32 * (it + 1))
                    for f in range(FC):
                        k = e * FC + f
                        blk = f // BLK
                        act.wait_ge(h_full, k + 1)
                        act.wait_ge(h_lo, k)
                        act.activation(h[:, f % 2, :], ps_h[:, f % 2, 0:CAP], ACT.Gelu, bias=b1[:, r, f:f + 1]
                                       ).then_inc(gelu_done, 1)
                        if blk < NBLK - 1 or has_next(last, r):
                            B, q = e * NBLK + blk + 1, (blk + 1) % 2
                            if f % BLK == 0:
                                use = (it * 2 + r) * (NBLK // 2) + (blk + 1) // 2
                                act.wait_ge(w1_in[q], 16 * (use + 1))
                                act.wait_ge(w2_in[q], 16 * (use + 1))
                                act.wait_ge(fc2_done, BLK * (B - 1) + 1)
                            split_hi(B, q, f % BLK)
                        if has_next(last, r) and f in TURN_AT:
                            for c in TURN_AT[f]:
                                token_hi(1 - r, c, DC * (e + 1) + c)

            each_pair(act, run)

        @block.vector
        def _(dve):
            def split_lo(q, piece, n_done):
                dve.wait_ge(w_hi, n_done + 1)
                n = 2 * (piece % 2)
                if piece < 2:
                    dve.tensor_tensor(w1s[:, q, LO, n:n + 2, :], w1[:, q, n:n + 2, :], raw(w1s[:, q, HI, n:n + 2, :]),
                                      ALU.subtract).then_inc(w_lo, 1)
                else:
                    dve.tensor_tensor(w2s[:, q, LO, n:n + 2, :], w2[:, q, n:n + 2, :], raw(w2s[:, q, HI, n:n + 2, :]),
                                      ALU.subtract).then_inc(w_lo, 1)

            def token_lo(r, c, cc):
                dve.wait_ge(xe_hi, cc + 1)
                dve.tensor_tensor(xe[:, r, LO, c, :], ps_t[:, c % 2, 0:CAP], raw(xe[:, r, HI, c, :]), ALU.subtract
                                  ).then_inc(xe_lo, 1)

            def read_gates(e, r, count):
                dve.wait_ge(gathered[r], 16 * CT * count)
                dve.tensor_copy(gates[:, r, :], xg[:, r, :, bass.ds(e + D, 1)].rearrange("p j a -> p (j a)")
                                ).then_inc(gate_ready, 1)

            dve.wait_ge(gelu_done, 2)
            dve.memset(h[:], 0.0).then_inc(h_lo, 1)
            dve.memset(gates[:], 0.0).then_inc(xe_lo, 1)
            for piece in range(PIECES):
                split_lo(0, piece, piece)
            for c in range(DC):
                token_lo(0, c, c)
            read_gates(0, 0, 1)

            def run(it, last):
                for r in range(2):
                    e = 2 * it + r
                    for f in range(FC):
                        k = e * FC + f
                        blk = f // BLK
                        dve.wait_ge(gelu_done, k + 3)
                        dve.wait_ge(fc2_done, k)
                        dve.tensor_copy(hs[:, f % 2, HI, :], h[:, f % 2, :]).then_inc(h_hi, 1)
                        dve.wait_ge(h_hi, k + 1)
                        dve.tensor_tensor(hs[:, f % 2, LO, :], h[:, f % 2, :], raw(hs[:, f % 2, HI, :]), ALU.subtract
                                          ).then_inc(h_lo, 1)
                        if blk < NBLK - 1 or has_next(last, r):
                            split_lo((blk + 1) % 2, f % BLK, (e * NBLK + blk + 1) * PIECES + f % BLK)
                        if has_next(last, r) and f in TURN_AT:
                            for c in TURN_AT[f]:
                                token_lo(1 - r, c, DC * (e + 1) + c)
                            if f == max(TURN_AT):
                                read_gates(e + 1, 1 - r, it + r + 1)
                    dve.wait_ge(fc2_done, FC * (e + 1) + 1)
                    dve.wait_ge(scattered, 16 * CT * e)
                    dve.wait_ge(gate_ready, e + 1)
                    for j in range(CT):
                        dve.tensor_tensor(out[:, j, 0:D], ps_y[:, j, :], b2[:, r, :], ALU.add).then_inc(y_copied, 1)
                    for j in range(CT):
                        dve.wait_ge(y_copied, CT * e + j + 1)
                        dve.tensor_copy(out[:, j, D:D + 1], gates[:, r, j:j + 1])
                        dve.tensor_scalar(out[:, j, 0:D], out[:, j, 0:D], gates[:, r, j:j + 1], None, ALU.mult
                                          ).then_inc(out_ready, 1)

            each_pair(dve, run)

        @block.tensor
        def _(pe):
            def turn(r, c, cc):
                pe.wait_ge(xe_lo, cc)
                for j in range(CT):
                    mm = pe.transpose(ps_t[:, c % 2, j * P:(j + 1) * P], xg[:, r, j, c * P:(c + 1) * P], ident[:])
                mm.then_inc(t_full, 1)

            def product(bank, pairs, first, final):
                for n, (a, b) in enumerate(pairs):
                    mm = pe.matmul(bank, a, b, start=(first and n == 0), stop=(final and n == len(pairs) - 1))
                return mm

            THREE = ((HI, HI), (LO, HI), (HI, LO))

            def fc1(e, r, f):
                k = e * FC + f
                blk, q = f // BLK, (f // BLK) % 2
                cols = slice((f % BLK) * P, (f % BLK + 1) * P)
                if f == 0:
                    pe.wait_ge(xe_lo, DC * (e + 1) + 1)
                if f % BLK == 0:
                    pe.wait_ge(w_lo, PIECES * (e * NBLK + blk) + 2)
                pe.wait_ge(gelu_done, k + 1)
                product(ps_h[:, f % 2, 0:CAP],
                        [(w1s[:, q, a, c, cols], xe[:, r, b, c, :]) for a, b in THREE for c in range(DC)],
                        True, True).then_inc(h_full, 1)

            def fc2(e, r, f):
                k = e * FC + f
                blk, q = f // BLK, (f // BLK) % 2
                if f == 0:
                    pe.wait_ge(y_copied, CT * e)
                if f % BLK == 0:
                    pe.wait_ge(w_lo, PIECES * (e * NBLK + blk) + 4)
                pe.wait_ge(h_lo, k + 2)
                for j in range(CT):
                    mm = product(ps_y[:, j, :],
                                 [(hs[:, f % 2, a, j * P:(j + 1) * P], w2s[:, q, b, f % BLK, :]) for a, b in THREE],
                                 f == 0, f == FC - 1)
                mm.then_inc(fc2_done, 1)

            pe.wait_ge(consts, 2)
            pe.wait_ge(gathered[0], 16 * CT)
            for c in range(DC):
                if c == 0:
                    pe.transpose(ps_t[:, 0, 0:P], ident[:], ident[:]).then_inc(fc2_done, 1)
                turn(0, c, c)

            def run(it, last):
                for r in range(2):
                    e = 2 * it + r
                    for f in range(FC):
                        fc1(e, r, f)
                        if f > 0:
                            fc2(e, r, f - 1)
                        if has_next(last, r) and f in TURN_AT:
                            if f == min(TURN_AT):
                                pe.wait_ge(gathered[1 - r], 16 * CT * (it + r + 1))
                            for c in TURN_AT[f]:
                                turn(1 - r, c, DC * (e + 1) + c)
                    fc2(e, r, FC - 1)

            each_pair(pe, run)


def build_final(nc, x1_dram, acc_dram, out_dram, NB):
    with ExitStack() as ctx:
        sb = lambda name, shape, dt=F32: ctx.enter_context(nc.sbuf_tensor(name, shape, dt))
        sem = lambda name: ctx.enter_context(nc.semaphore(name))
        acc = sb("f_acc", [P, 2, QT, ACC])
        x1 = sb("f_x1", [P, 2, QT, D])
        z = sb("f_z", [P, 2, QT, D])
        sums = sb("f_sums", [P, 4, QT])
        stats = sb("f_stats", [P, QT, 6])
        mv = sb("f_mv", [P, 2, QT, 2])
        std = sb("f_std", [P, 2, QT])
        rstd = sb("f_rstd", [P, QT])
        eps = sb("f_eps", [P, 1])
        passed = sem("f_passed")
        a_in = [sem(f"f_in{u}") for u in range(2)]
        z_out = [sem(f"f_out{u}") for u in range(2)]
        consts, d, mv_ready, std_ready, z_ready = (sem("f_consts"), sem("f_dve_step"), sem("f_mv_ready"),
                                                   sem("f_std_ready"), sem("f_z_ready"))
        block = ctx.enter_context(nc.Block())
        tokens = lambda dram, it, u: dram[bass.ds(it * T + u * HALF, HALF), :].rearrange("(t p) d -> p t d", p=P)

        @block.sync
        def _(sp):
            with sp.Fori(0, NB) as it:
                for u in range(2):
                    sp.wait_ge(mv_ready, 2 * it)
                    sp.dma_start(acc[:, u], tokens(acc_dram, it, u)).then_inc(a_in[u], 16)
                    sp.dma_start(x1[:, u], tokens(x1_dram, it, u)).then_inc(a_in[u], 16)
            for u in range(2):
                sp.wait_ge(z_out[u], 16 * NB)

        @block.gpsimd
        def _(pool):
            pool.memset(eps[:], EPS).then_inc(consts, 1)

        @block.scalar
        def _(act):
            act.wait_ge(consts, 1)
            with act.Fori(0, NB) as it:
                for u in range(2):
                    n = 2 * it + u
                    act.wait_ge(mv_ready, n + 1)
                    act.activation(std[:, u, :], mv[:, u, :, 1], ACT.Sqrt, bias=eps[:]).then_inc(std_ready, 1)
                    act.wait_ge(z_ready, n + 1)
                    act.dma_start(tokens(out_dram, it, u), z[:, u]).then_inc(z_out[u], 16)

        @block.vector
        def _(dve):
            PER = 7
            with dve.Fori(0, NB) as it:
                for u in range(2):
                    n = 2 * it + u
                    done = n * PER
                    gsum = acc[:, u, :, D]
                    dve.wait_ge(a_in[u], 32 * (it + 1))
                    dve.tensor_scalar(sums[:, 0], gsum, 0.0, None, ALU.is_gt).then_inc(d, 1)
                    dve.wait_ge(d, done + 1)
                    dve.tensor_scalar(sums[:, 1], sums[:, 0], -1.0, 1.0, ALU.mult, ALU.add).then_inc(d, 1)
                    dve.wait_ge(d, done + 2)
                    dve.tensor_tensor(sums[:, 2], sums[:, 1], gsum, ALU.add).then_inc(d, 1)
                    dve.wait_ge(d, done + 3)
                    dve.reciprocal(sums[:, 3], sums[:, 2]).then_inc(d, 1)
                    dve.wait_ge(d, done + 4)
                    dve.wait_ge(z_out[u], 16 * it)
                    for t in range(QT):
                        ins = dve.scalar_tensor_tensor(out=z[:, u, t, :], in0=acc[:, u, t, 0:D],
                                                       scalar=sums[:, 3, t:t + 1], in1=x1[:, u, t, :],
                                                       op0=ALU.mult, op1=ALU.add)
                    ins.then_inc(d, 1)
                    dve.wait_ge(d, done + 5)
                    for t in range(QT):
                        ins = dve.bn_stats(stats[:, t, :], z[:, u, t, :])
                    ins.then_inc(d, 1)
                    plain(dve, d, done + 6, passed)
                    for t in range(QT):
                        ins = dve.bn_aggr(mv[:, u, t, :], stats[:, t, :])
                    ins.then_inc(mv_ready, 1)
                    dve.wait_ge(std_ready, n + 1)
                    dve.reciprocal(rstd[:], std[:, u, :]).then_inc(d, 1)
                    dve.wait_ge(d, done + 7)
                    for t in range(QT):
                        ins = dve.tensor_scalar(z[:, u, t, :], z[:, u, t, :], mv[:, u, t, 0:1], rstd[:, t:t + 1],
                                                ALU.subtract, ALU.mult)
                    ins.then_inc(z_ready, 1)


def build_program(nc, x, xT, w, out, NB):
    N = NB * T
    scratch = {"wqk": nc.dram_tensor("scratch_wqk", [GROUPS, P, 4 * DC * P], F32).ap()}
    x1_dram = nc.dram_tensor("scratch_x1", [N, D], F32).ap()
    table = nc.dram_tensor("scratch_table", [N, TABLE], F32).ap()
    acc_dram = nc.dram_tensor("scratch_sums", [N, ACC], F32).ap()
    logits_dram = nc.dram_tensor("scratch_logits", [E_N, N], F32).ap()
    list_dram = nc.dram_tensor("scratch_lists", [E_N, N // E_N], U32).ap()
    with ExitStack() as ctx:
        sb = lambda name, shape, dt=F32: ctx.enter_context(nc.sbuf_tensor(name, shape, dt))
        keep = {"wo": sb("wo_cols", [P, DC, D]), "wv": sb("wv_parts", [P, 2, DC, D], F32R),
                "bq": sb("bq_folded", [P, GROUPS]), "bk": sb("bk_cols", [P, GROUPS]), "bo": sb("bo_folded", [P, D])}
        build_weights(nc, w, scratch, keep)
        build_attention(nc, x, xT, x1_dram, scratch, keep, NB)
    with ExitStack() as ctx:
        logits = ctx.enter_context(nc.sbuf_tensor("logits_t", [E_N, N], F32))
        build_router(nc, x1_dram, w, table, logits_dram, acc_dram, logits, NB)
        build_selection(nc, table, logits_dram, list_dram, logits, NB)
    build_experts(nc, w, table, list_dram, acc_dram, NB)
    build_final(nc, x1_dram, acc_dram, out, NB)


def kernel(**inputs):
    import concourse.bacc as _bacc
    from concourse.bass_utils import run_bass_kernel_spmd as _run

    attn = lambda name: np.asarray(inputs["L0_attn_" + name])
    ffn = lambda name: np.asarray(inputs["L0_ffn_" + name])
    B, S, _ = attn("x").shape
    x = attn("x").reshape(B * S, D)
    layout = {
        "x": x, "xT": x.T,
        "Wq": attn("Wq"), "WkT": attn("Wk").T, "WvT": attn("Wv").T, "WoT": attn("Wo").T,
        "bq": attn("bq"), "bk": attn("bk"), "bv": attn("bv"), "bo": attn("bo"),
        "LqT": attn("Wq_lsr").transpose(0, 2, 1), "LkT": attn("Wk_lsr").transpose(0, 2, 1),
        "norm": ffn("norm_weight"), "rwT": ffn("router_weight").T, "rb": ffn("router_bias"),
        "w1T": ffn("fc1_weight").transpose(0, 2, 1), "w2T": ffn("fc2_weight").transpose(0, 2, 1),
        "b1T": ffn("fc1_bias").reshape(E_N, FC, P).transpose(0, 2, 1), "b2": ffn("fc2_bias"),
    }
    nc = _bacc.Bacc("TRN2", target_bir_lowering=False, num_devices=1)
    arrays = {"in_" + k: np.ascontiguousarray(a) for k, a in layout.items()}
    w = {k: nc.dram_tensor("in_" + k, arrays["in_" + k].shape, mybir.dt.from_np(arrays["in_" + k].dtype),
                           kind="ExternalInput").ap() for k in layout}
    out = nc.dram_tensor("out_x", (B * S, D), F32, kind="ExternalOutput").ap()
    build_program(nc, w["x"], w["xT"], w, out, B)
    r = _run(nc, [arrays], core_ids=[0])
    return r.results[0]["out_x"].reshape(B, S, D)
```

```python
from contextlib import ExitStack

import numpy as np
import concourse.bass as bass
from concourse import mybir

F32 = mybir.dt.float32
F32R = mybir.dt.float32r
BF16 = mybir.dt.bfloat16
I32 = mybir.dt.int32
U32 = mybir.dt.uint32
ALU = mybir.AluOpType
ACT = mybir.ActivationFunctionType
AX = mybir.AxisListType

P = 128
D = 512
DC = D // P
HEADS = 16
DH = 32
HG = P // DH
GROUPS = HEADS // HG
T = 1024
TT = T // P
HALF = 512
EPS = 1e-5
SCALE = 1.0 / float(np.sqrt(DH))
MASKED = -(2.0 ** 120)
ACC = D + 4
HI, LO = 0, 1

Q_STRIPS = (HI, LO, HI)
K_STRIPS = (HI, HI, LO)
MAX_STRIP = 96


def raw(ap):
    return ap.bitcast(F32)


def plain(eng, semaphore, value, passed):
    eng.wait_ge(semaphore, value)
    eng.sem_inc(passed, 1)


def build_weights(nc, w, scratch, keep):
    with ExitStack() as ctx:
        sb = lambda name, shape, dt=F32: ctx.enter_context(nc.sbuf_tensor(name, shape, dt))
        sem = lambda name: ctx.enter_context(nc.semaphore(name))
        lq = sb("lq_blocks", [P, GROUPS, P])
        lk = sb("lk_blocks", [P, GROUPS, P])
        fold = sb("fold", [P, GROUPS, P])
        wq = sb("wq_rows", [P, GROUPS, D])
        wqf = sb("wq_folded", [P, GROUPS, DC, P])
        wk = sb("wk_cols", [P, DC, GROUPS, P])
        wv = sb("wv_cols", [P, DC, D])
        parts = sb("qk_parts", [P, GROUPS, 4, DC, P], F32R)
        bq = sb("bq_cols", [P, GROUPS])
        bv = sb("bv_cols", [P, GROUPS])
        bv_wide = sb("bv_wide", [P, GROUPS, P])
        bo = sb("bo_rows", [P, D])
        ones = sb("setup_ones", [P, P])
        ps_fold = ctx.enter_context(nc.psum_tensor("ps_fold", [P, GROUPS, P], F32))
        ps_wq = ctx.enter_context(nc.psum_tensor("ps_wq", [P, GROUPS, DC * P], F32))
        ps_bias = ctx.enter_context(nc.psum_tensor("ps_bias", [P, HALF], F32))
        ps_bo = ctx.enter_context(nc.psum_tensor("ps_bo", [P, D], F32))
        zeroed, blocks_in, in_q, in_rest = sem("zeroed"), sem("blocks_in"), sem("in_q"), sem("in_rest")
        fold_mm, folded, wq_mm, bias_done = sem("fold_mm"), sem("folded"), sem("wq_mm"), sem("bias_done")
        copied, split_hi, split_lo, stored = sem("copied"), sem("split_hi"), sem("split_lo"), sem("stored")
        wide, bo_mm, wk_in, wv_in, v_hi = sem("wide"), sem("bo_mm"), sem("wk_in"), sem("wv_in"), sem("v_hi")
        block = ctx.enter_context(nc.Block())

        @block.sync
        def _(sp):
            sp.wait_ge(zeroed, 2)
            for r in range(HG):
                rows = slice(DH * r, DH * r + DH)
                for blocks, name in ((lq, "LqT"), (lk, "LkT")):
                    sp.dma_start(blocks[rows, :, rows], w[name].rearrange("(g r) a b -> r a g b", r=HG)[r]
                                 ).then_inc(blocks_in, 16)
            sp.dma_start(wq[:], w["Wq"].rearrange("(g p) d -> p g d", p=P)).then_inc(in_q, 16)
            sp.dma_start(wk[:], w["WkT"].rearrange("(c p) (g n) -> p c g n", p=P, n=P)).then_inc(wk_in, 16)
            sp.dma_start(wv[:], w["WvT"].rearrange("(c p) n -> p c n", p=P)).then_inc(wv_in, 16)
            with nc.allow_non_contiguous_dma(reason="small bias columns"):
                sp.dma_start(bq[:], w["bq"].rearrange("(g p) -> p g", p=P)).then_inc(in_q, 16)
                sp.dma_start(bv[:], w["bv"].rearrange("(g p) -> p g", p=P)).then_inc(in_rest, 16)
                sp.dma_start(keep["bk"][:], w["bk"].rearrange("(g p) -> p g", p=P)).then_inc(in_rest, 16)
            sp.dma_start(keep["wo"][:], w["WoT"].rearrange("(c p) n -> p c n", p=P)).then_inc(in_rest, 16)
            sp.dma_start(bo[:], w["bo"].rearrange("(a n) -> a n", a=1).to_broadcast([P, D])).then_inc(in_rest, 16)
            sp.wait_ge(split_hi, 2)
            sp.wait_ge(split_lo, 2)
            sp.dma_start(scratch["wqk"].rearrange("g p k -> p g k"),
                         raw(parts[:]).rearrange("p g k c n -> p g (k c n)")).then_inc(stored, 16)
            sp.wait_ge(stored, 16)

        @block.gpsimd
        def _(pool):
            pool.memset(lq[:], 0.0).then_inc(zeroed, 1)
            pool.memset(lk[:], 0.0).then_inc(zeroed, 1)

        @block.tensor
        def _(pe):
            pe.wait_ge(blocks_in, 16 * 2 * HG)
            for g in range(GROUPS):
                mm = pe.matmul(ps_fold[:, g, :], lq[:, g, :], lk[:, g, :], start=True, stop=True)
            mm.then_inc(fold_mm, 1)
            pe.wait_ge(folded, 1)
            pe.wait_ge(in_q, 32)
            for g in range(GROUPS):
                for c in range(DC):
                    mm = pe.matmul(ps_wq[:, g, c * P:(c + 1) * P], wq[:, g, c * P:(c + 1) * P], fold[:, g, :],
                                   start=True, stop=True)
                mm.then_inc(wq_mm, 1)
            for g in range(GROUPS):
                mm = pe.matmul(ps_bias[:, g:g + 1], fold[:, g, :], bq[:, g:g + 1], start=True, stop=True)
            mm.then_inc(bias_done, 1)
            pe.wait_ge(wide, 2)
            pe.wait_ge(in_rest, 64)
            for c in range(DC):
                mm = pe.matmul(ps_bo[:], bv_wide[:, c, :], keep["wo"][:, c, :], start=(c == 0), stop=(c == DC - 1))
            mm.then_inc(bo_mm, 1)

        @block.vector
        def _(dve):
            dve.memset(ones[:], 1.0).then_inc(wide, 1)
            dve.wait_ge(fold_mm, 1)
            dve.tensor_copy(fold[:], ps_fold[:]).then_inc(folded, 1)
            dve.wait_ge(wk_in, 16)
            dve.tensor_copy(parts[:, :, 2], wk[:].rearrange("p c g n -> p g c n")).then_inc(split_hi, 1)
            for g in range(GROUPS):
                dve.wait_ge(wq_mm, g + 1)
                dve.tensor_copy(wqf[:, g], ps_wq[:, g, :].rearrange("p (c n) -> p c n", c=DC)).then_inc(copied, 1)
            dve.wait_ge(copied, GROUPS)
            dve.tensor_copy(parts[:, :, 0], wqf[:]).then_inc(split_hi, 1)
            dve.wait_ge(split_hi, 2)
            for g in range(GROUPS):
                dve.tensor_tensor(parts[:, g, 1], wqf[:, g], raw(parts[:, g, 0]), ALU.subtract)
                ins = dve.tensor_tensor(parts[:, g, 3], wk[:, :, g, :], raw(parts[:, g, 2]), ALU.subtract)
            ins.then_inc(split_lo, 2)
            dve.wait_ge(bias_done, 1)
            dve.tensor_copy(keep["bq"][:], ps_bias[:, 0:GROUPS]).then_inc(copied, 1)
            dve.wait_ge(in_rest, 64)
            for g in range(GROUPS):
                ins = dve.tensor_scalar(bv_wide[:, g, :], ones[:], bv[:, g:g + 1], None, ALU.mult)
            ins.then_inc(wide, 1)
            dve.wait_ge(v_hi, 1)
            dve.tensor_tensor(keep["wv"][:, LO], wv[:], raw(keep["wv"][:, HI]), ALU.subtract).then_inc(split_lo, 1)
            dve.wait_ge(bo_mm, 1)
            dve.tensor_tensor(keep["bo"][:], ps_bo[:], bo[:], ALU.add).then_inc(split_lo, 1)

        @block.scalar
        def _(act):
            act.wait_ge(wv_in, 16)
            act.activation(keep["wv"][:, HI], wv[:], ACT.Copy).then_inc(v_hi, 1)


def plan_batch():
    order = [("v", t) for t in range(TT)]
    for g in range(GROUPS):
        order += plan_step(g, True)
    order += [("out", t) for t in range(TT)]
    e = len(attend_steps())
    for g in range(GROUPS):
        n = order.index(("values", g, e - 1))
        order[n:n + 3] = [order[n + 2], order[n], order[n + 1]]
    return order


def attend_steps():
    return [(hh, j, max(0, j * P - hh * HALF)) for hh in range(2) for j in range(4 * hh + 4)]


def max_steps():
    out = []
    for h in range(HG):
        out += [(h, it, it, 0, (it + 1) * P) for it in range(4)]
        out += [(h, it, it, 0, HALF) for it in range(4, TT)]
        out += [(h, it + 4, it, HALF, (it + 1) * P - HALF) for it in range(4, TT)]
    return out


PROB_BUFS = 4
DEN_PIECES = 4
LEAD = 3
TAIL = 4


def attend_parts(g, k, e):
    parts = [("scores", g, k, 0), ("scores", g, k, 1)]
    for n in ([k - 1] if k > 0 else []) + ([k] if k == e - 1 else []):
        parts += [("values", g, n), ("sums", g, n)]
    return parts


def plan_step(g, attend):
    order = [("proj", g, i) for i in range(4)]
    e, m = len(attend_steps()) if attend else 0, len(max_steps())
    if not attend:
        return order + [("max", g, i) for i in range(m)] + [("maxT", g)]
    parts = [part for k in range(e) for part in attend_parts(g, k, e)]
    first, final = parts.index(("scores", g, LEAD, 0)), len(parts) - TAIL
    done = 0
    for n, part in enumerate(parts):
        order.append(part)
        if first <= n < final:
            share = m * (n + 1 - first) // (final - first)
            order += [("max", g, i) for i in range(done, share)]
            done = share
        if n == len(parts) - 3:
            order.append(("maxT", g))
    assert done == m
    return order


def build_attention(nc, x_dram, xT_dram, x1_dram, acc_dram, scratch, keep, NB):
    with ExitStack() as ctx:
        sb = lambda name, shape, dt=F32: ctx.enter_context(nc.sbuf_tensor(name, shape, dt))
        ps = lambda name, shape, dt=F32: ctx.enter_context(nc.psum_tensor(name, shape, dt))
        sem = lambda name: ctx.enter_context(nc.semaphore(name))

        xs = sb("x_parts", [P, 2, DC, T], F32R)
        wqk = sb("wqk_group", [P, 4, DC, P], F32R)
        nat = sb("natural", [P, 4, T])
        q_ops = sb("q_operands", [P, 2, HG, T], F32R)
        k_ops = sb("k_operands", [P, 2, HG, T], F32R)
        v = sb("v_rows", [P, TT, D])
        y = sb("y_cols", [P, GROUPS, T])
        probs = sb("probs", [P, PROB_BUFS, 2, HALF])
        mx = sb("max_slots", [P, HG, 12])
        mrow = sb("row_max", [P, HG, TT])
        mneg = sb("minus_max", [HG * TT, 2, P], F32R)
        den = sb("denominators", [P, HALF])
        xres = sb("x_residual", [P, 2, D])
        x1 = sb("x1_tile", [P, 2, D])
        stats = sb("ln_stats", [P, TT, 6])
        mv = sb("ln_mv", [P, 2, 2])
        std = sb("ln_std", [P, 2])
        rstd = sb("ln_rstd", [P, 2])
        eps = sb("eps_tile", [P, 1])
        ones = sb("ones_f32", [P, DH])
        zeros = sb("zeros_f32", [P, ACC // 4])
        ident = sb("ident_f32", [P, P])
        identb = sb("ident_bf16", [P, P], BF16)
        mask_q = sb("mask_q_rows", [P, P], BF16)
        mask_k = sb("mask_k_rows", [P, P], BF16)

        shared = ps("shared_banks", [P, 2, HALF])
        st = ps("scores_t", [P, 2, 2, HALF])
        yb = ps("y_bank", [P, HALF])
        db = ps("den_bank", [P, HALF])

        bank_full = [sem(f"bank{k}_full") for k in range(2)]
        bank_free = [sem(f"bank{k}_free") for k in range(2)]
        consts, strip_zero, strips_filled, own_zeros, ident_ready = sem("consts"), sem("strip_zero"), sem("strips_filled"), sem("own_zeros"), sem("ident_ready")
        x_in, x_split, w_in = sem("x_in"), sem("x_split"), sem("w_in")
        hi_ready, first_hi = sem("hi_ready"), sem("first_hi")
        zeros_ready, cleared = sem("zeros_ready"), sem("cleared")
        sp_passed, pool_passed, dve_passed = sem("sp_passed"), sem("pool_passed"), sem("dve_passed")
        strips_sent = [sem(f"strips_sent{h}") for h in range(HG)]
        st_full, exp_done, pv_done, normed = sem("st_full"), sem("exp_done"), sem("pv_done"), sem("normed")
        y_drained, den_drained, rden_ready = sem("y_drained"), sem("den_drained"), sem("rden_ready")
        mx_joined, mneg_hi, m_sent = sem("mx_joined"), sem("mneg_hi"), sem("m_sent")
        res_in, x1_out = [sem(f"res_in{r}") for r in range(2)], [sem(f"x1_out{r}") for r in range(2)]
        bo_added, summed, stats_ready, mv_ready, std_ready, rstd_ready, x1_ready = (
            sem("bo_added"), sem("summed"), sem("stats_ready"), sem("mv_ready"), sem("std_ready"),
            sem("rstd_ready"), sem("x1_ready"))

        N_CONSTS = 6
        STRIPS = 16 * 2 * len(Q_STRIPS)
        steps, maxes = attend_steps(), max_steps()
        NE, NM = len(steps), len(maxes)
        batch = plan_batch()
        lead_in = plan_step(GROUPS - 1, False)
        uses_bank = lambda item: item[0] not in ("scores", "values", "sums")
        N_LEAD = sum(map(uses_bank, lead_in))
        N_BATCH = sum(map(uses_bank, batch))
        N_LAST = N_BATCH - 4 - NM - 1
        assert N_BATCH % 2 == 0

        def slot_of(k, pair):
            return (2 * k + pair) % PROB_BUFS

        assert PROB_BUFS == 4 and (2 * NE) % PROB_BUFS == 0

        def ends_half(item):
            return item[0] == "sums" and steps[item[2]][1] == 4 * steps[item[2]][0] + 3

        def turns(order, base):
            at, n = {}, base
            for item in order:
                if uses_bank(item):
                    at[item] = (n % 2, n // 2)
                    n += 1
            return at

        lead_turns = turns(lead_in, 0)
        batch_turns = turns(batch, N_LEAD)
        last = [i for i in batch if not (i[0] in ("proj", "max", "maxT") and i[1] == GROUPS - 1)]
        last_turns = turns(last, N_LEAD)

        def scope(b, lead=False):
            if lead:
                return lead_in, lead_turns, 0
            if isinstance(b, int) and b == NB - 1:
                return last, last_turns, b * (N_BATCH // 2)
            return batch, batch_turns, b * (N_BATCH // 2)

        def await_parts(eng, passed, b, g, lead=False):
            _, at, off = scope(b, lead)
            for i in (2, 3):
                bank, turn = at[("proj", g, i)]
                plain(eng, bank_free[bank], off + turn + 1, passed)

        def each_batch(eng, run):
            if NB > 1:
                with eng.Fori(0, NB - 1) as b:
                    run(b)
            run(NB - 1)

        block = ctx.enter_context(nc.Block())

        @block.sync
        def _(sp):
            def load_x(b, n):
                for h in range(HG):
                    sp.wait_ge(strips_sent[h], n * STRIPS)
                sp.dma_start(nat[:], xT_dram.rearrange("(c p) t -> p c t", p=P)[:, :, bass.ds(b * T, T)]
                             ).then_inc(x_in, 16)

            def load_w(g):
                sp.dma_start(raw(wqk[:]), scratch["wqk"][g].rearrange("p (k c n) -> p k c n", k=4, c=DC)).then_inc(w_in, 16)

            def strips(b, g, lead=False):
                await_parts(sp, sp_passed, b, (g - 1) % GROUPS, lead)
                for h in range(HG):
                    src = slice(DH * h, DH * h + DH)
                    for s in range(3):
                        dst = slice(DH * s, DH * s + DH)
                        sp.dma_start(raw(q_ops[dst, g % 2, h, :]), nat[src, Q_STRIPS[s], :]).then_inc(strips_sent[h], 16)
                        sp.dma_start(raw(k_ops[dst, g % 2, h, :]), nat[src, 2 + K_STRIPS[s], :]).then_inc(strips_sent[h], 16)

            def run(b):
                n0 = b * GROUPS
                more = not (isinstance(b, int) and b == NB - 1)
                for g in range(GROUPS - 1):
                    load_w(g + 1)
                    strips(b, g + 1)
                    if g == 0:
                        sp.dma_start(acc_dram[bass.ds(b * T, T), :].rearrange("(p t) (q a) -> p (t q) a", p=P, q=4),
                                     zeros[:].rearrange("p (o a) -> p o a", o=1).to_broadcast([P, 4 * TT, ACC // 4])
                                     ).then_inc(cleared, 16)
                if more:
                    load_x(b + 1, n0 + GROUPS)
                    load_w(0)
                    strips(b, 0)
                for t in range(TT):
                    sp.wait_ge(summed, b * TT + max(t - 1, 0))
                    sp.dma_start(xres[:, t % 2], x_dram[bass.ds(b * T + t * P, P), :]).then_inc(res_in[t % 2], 16)
                    if t >= 2:
                        store(b, t - 2)
                store(b, TT - 2)
                store(b, TT - 1)

            def store(b, t):
                sp.wait_ge(x1_ready, b * TT + t + 1)
                sp.dma_start(x1_dram[bass.ds(b * T + t * P, P), :], x1[:, t % 2]).then_inc(x1_out[t % 2], 16)

            load_x(0, 0)
            load_w(0)
            strips(0, 0, True)
            sp.wait_ge(zeros_ready, 1)
            each_batch(sp, run)
            for r in range(2):
                sp.wait_ge(x1_out[r], 16 * TT // 2 * NB)
            sp.wait_ge(cleared, 16 * NB)

        @block.gpsimd
        def _(pool):
            pool.memset(eps[:], EPS).then_inc(consts, 1)
            pool.memset(ones[:], 1.0).then_inc(consts, 1)
            pool.memset(zeros[:], 0.0).then_inc(zeros_ready, 1)
            pool.memset(ident[:], 0.0).then_inc(own_zeros, 1)
            pool.memset(mask_q[:], 0.0).then_inc(own_zeros, 1)
            pool.memset(mask_k[:], 0.0).then_inc(own_zeros, 1)
            pool.wait_ge(own_zeros, 3)
            pool.affine_select(out=ident[:], in_=ident[:], compare_op=ALU.not_equal, fill=1.0, base=0,
                               pattern=[[-1, P]], channel_multiplier=1).then_inc(ident_ready, 1)
            pool.wait_ge(ident_ready, 1)
            pool.tensor_copy(identb[:], ident[:]).then_inc(consts, 2)
            pool.affine_select(out=mask_q[:], in_=mask_q[:], compare_op=ALU.is_ge, fill=MASKED, base=0,
                               pattern=[[-1, P]], channel_multiplier=1).then_inc(consts, 1)
            pool.affine_select(out=mask_k[:], in_=mask_k[:], compare_op=ALU.is_ge, fill=MASKED, base=0,
                               pattern=[[1, P]], channel_multiplier=-1).then_inc(consts, 1)

            def split_x(n):
                await_parts(pool, pool_passed, n - 1, GROUPS - 2)
                plain(pool, x_in, 16 * (n + 1), pool_passed)
                for c in range(DC):
                    ins = pool.tensor_copy(xs[:, HI, c, :], nat[:, c, :])
                ins.then_inc(x_split, 1)
                pool.wait_ge(x_split, 2 * n + 1)
                for c in range(DC):
                    ins = pool.tensor_tensor(xs[:, LO, c, :], nat[:, c, :], raw(xs[:, HI, c, :]), ALU.subtract)
                ins.then_inc(x_split, 1)

            def normalise(b, g, hh):
                n = 2 * (b * GROUPS + g) + hh
                half = y[:, g, hh * HALF:(hh + 1) * HALF]
                plain(pool, y_drained, n + 1, pool_passed)
                pool.wait_ge(rden_ready, DEN_PIECES * (n + 1))
                pool.tensor_tensor(half, half, den[:], ALU.mult).then_inc(normed, 1)

            def run(b):
                order, _, _ = scope(b)
                for item in order:
                    if ends_half(item) and item[1:] != (GROUPS - 1, NE - 1):
                        normalise(b, item[1], steps[item[2]][0])
                    if item == ("proj", GROUPS - 2, 3) and not (isinstance(b, int) and b == NB - 1):
                        split_x(b + 1)
                    if item[0] != "out":
                        continue
                    t = item[1]
                    pool.wait_ge(res_in[t % 2], 16 * (b * (TT // 2) + t // 2 + 1))
                    pool.tensor_tensor(xres[:, t % 2], xres[:, t % 2], keep["bo"][:], ALU.add).then_inc(bo_added, 1)
                    if t == 2:
                        normalise(b, GROUPS - 1, 1)

            pool.memset(den[:], 0.0).then_inc(normed, 1)
            pool.wait_ge(normed, 1)
            pool.memset(raw(k_ops[MAX_STRIP:P]), 0.0).then_inc(strip_zero, 1)
            pool.wait_ge(strip_zero, 1)
            pool.memset(raw(k_ops[MAX_STRIP:MAX_STRIP + 2]), 1.0).then_inc(strips_filled, 1)
            pool.wait_ge(strips_filled, 1)
            pool.memset(raw(q_ops[MAX_STRIP:P]), 0.0).then_inc(strips_filled, 1)
            pool.wait_ge(strips_filled, 2)
            each_batch(pool, run)

        @block.tensor
        def _(pe):
            def take(bank, turn, off):
                pe.wait_ge(bank_free[bank], off + turn)

            def run(b, lead=False):
                order, at, off = scope(b, lead)
                nxt = 0 if lead else b * GROUPS + 1
                for item in order:
                    kind = item[0]
                    if kind == "scores":
                        scores(b, *item[1:])
                        continue
                    if kind == "values":
                        values(b, *item[1:])
                        continue
                    if kind == "sums":
                        if steps[item[2]][1] == 0:
                            pe.wait_ge(den_drained, 2 * (b * GROUPS + item[1]) + steps[item[2]][0])
                        weigh(item[2], db, lambda h, j: ones[:]).then_inc(pv_done, 1)
                        continue
                    bank, turn = at[item]
                    out = shared[:, bank, :]
                    if kind == "maxT":
                        pe.wait_ge(mx_joined, 2 if lead else 2 * (nxt + item[1] + 1))
                    take(bank, turn, off)
                    if kind == "v":
                        t = item[1]
                        if t == 0:
                            pe.wait_ge(x_split, 2 * (b + 1))
                        mm = product(out, [(xs[:, a, c, t * P:(t + 1) * P], keep["wv"][:, w, c, :])
                                           for a, w in ((HI, HI), (LO, HI), (HI, LO)) for c in range(DC)])
                        mm.then_inc(bank_full[bank], 1)
                    elif kind == "proj":
                        g, i = item[1], item[2]
                        if i == 0:
                            pe.wait_ge(w_in, 16 * (1 if lead else nxt + g + 1))
                            if lead:
                                pe.wait_ge(x_split, 2)
                            elif g == GROUPS - 1:
                                pe.wait_ge(x_split, 2 * (b + 2))
                        which, hh = i // 2, i % 2
                        mm = product(out, [(wqk[:, 2 * which + w, c, :], xs[:, a, c, hh * HALF:(hh + 1) * HALF])
                                           for a, w in ((HI, HI), (LO, HI), (HI, LO)) for c in range(DC)])
                        mm.then_inc(bank_full[bank], 1)
                    elif kind == "max":
                        g, (h, _, it, k0, n) = item[1], maxes[item[2]]
                        if item[2] % 12 == 0:
                            pe.wait_ge(strips_sent[h], (1 if lead else nxt + g + 1) * STRIPS)
                        buf = (g + 1) % 2
                        diag = k0 + n == (it + 1) * P
                        mm = pe.matmul(out[:, 0:n], q_ops[0:MAX_STRIP, buf, h, it * P:(it + 1) * P],
                                       k_ops[0:MAX_STRIP, buf, h, k0:k0 + n], start=True, stop=not diag)
                        if diag:
                            mm = pe.matmul(out[:, n - P:n], identb[:], mask_q[:], start=False, stop=True)
                        mm.then_inc(bank_full[bank], 1)
                    elif kind == "maxT":
                        pe.transpose(out[0:HG * TT, 0:P], mrow[:].rearrange("p h t -> p (h t)"), ident[:]
                                     ).then_inc(bank_full[bank], 1)
                    elif kind == "out":
                        t = item[1]
                        if t % (TT // 2) == 0:
                            pe.wait_ge(normed, 2 * GROUPS * (b + 1) + t // (TT // 2))
                        mm = product(out, [(y[:, c, t * P:(t + 1) * P], keep["wo"][:, c, :]) for c in range(DC)])
                        mm.then_inc(bank_full[bank], 1)

            def product(out, pairs):
                for n, (a, c) in enumerate(pairs):
                    mm = pe.matmul(out, a, c, start=(n == 0), stop=(n == len(pairs) - 1))
                return mm

            def scores(b, g, k, pair):
                hh, j, c0 = steps[k]
                buf = g % 2
                s = (b * GROUPS + g) * NE + k
                if k == 0 and pair == 0:
                    pe.wait_ge(m_sent, 32 * (b * GROUPS + g + 1))
                pe.wait_ge(exp_done, 2 * s + pair + 1)
                for q in range(2):
                    h = 2 * pair + q
                    out = st[:, pair, q, :]
                    diag = j * P >= hh * HALF
                    mm = pe.matmul(out[:, c0:HALF], k_ops[:, buf, h, j * P:(j + 1) * P],
                                   q_ops[:, buf, h, hh * HALF + c0:(hh + 1) * HALF], start=True, stop=not diag)
                    if diag:
                        mm = pe.matmul(out[:, c0:c0 + P], identb[:], mask_k[:], start=False, stop=True)
                mm.then_inc(st_full, 1)

            def values(b, g, k):
                hh, j, c0 = steps[k]
                s = (b * GROUPS + g) * NE + k
                if g == 0 and k == 0:
                    _, at, off = scope(b)
                    for t in (TT - 2, TT - 1):
                        bank, turn = at[("v", t)]
                        pe.wait_ge(bank_free[bank], off + turn + 1)
                if j == 0:
                    pe.wait_ge(y_drained, 2 * (b * GROUPS + g) + hh)
                pe.wait_ge(exp_done, 2 * s + 4)
                weigh(k, yb, lambda h, j: v[:, j, g * P + h * DH:g * P + (h + 1) * DH])

            def weigh(k, bank, rows):
                hh, j, c0 = steps[k]
                for h in range(HG):
                    mm = pe.matmul(bank[h * DH:(h + 1) * DH, c0:HALF], rows(h, j),
                                   probs[:, slot_of(k, h // 2), h % 2, c0:HALF],
                                   start=(j == 0), stop=(j == 4 * hh + 3), tile_position=(0, h * DH))
                return mm

            pe.wait_ge(consts, N_CONSTS)
            run(0, lead=True)
            each_batch(pe, run)

        @block.scalar
        def _(act):
            def run(b, lead=False):
                order, at, off = scope(b, lead)
                for item in order:
                    kind = item[0]
                    if kind == "scores":
                        exps(b, *item[1:])
                    if ends_half(item):
                        drain(b, item[1], steps[item[2]][0], item[2])
                    if not uses_bank(item):
                        continue
                    bank, turn = at[item]
                    src = shared[:, bank, :]
                    if kind == "v":
                        act.wait_ge(bank_full[bank], off + turn + 1)
                        act.activation(v[:, item[1], :], src, ACT.Copy).then_inc(bank_free[bank], 1)
                    elif kind == "proj":
                        g, i = item[1], item[2]
                        which, hh = i // 2, i % 2
                        act.wait_ge(bank_full[bank], off + turn + 1)
                        if i == 0:
                            if lead:
                                act.wait_ge(x_split, 2)
                            elif g == GROUPS - 1:
                                act.wait_ge(x_split, 2 * (b + 2))
                            if not lead:
                                for h in range(HG):
                                    act.wait_ge(strips_sent[h], (b * GROUPS + g + 1) * STRIPS)
                        gn = (g + 1) % GROUPS
                        bias = (keep["bq"], keep["bk"])[which]
                        act.activation(nat[:, 2 * which + HI, hh * HALF:(hh + 1) * HALF].bitcast(F32R), src,
                                       ACT.Identity, bias=bias[:, gn:gn + 1]).then_inc(hi_ready, 1)
                    elif kind == "maxT":
                        act.wait_ge(bank_full[bank], off + turn + 1)
                        n = 0 if lead else b * GROUPS + item[1] + 1
                        if lead:
                            act.wait_ge(strips_filled, 2)
                        else:
                            act.wait_ge(m_sent, 32 * n)
                        act.activation(mneg[:, HI, :], src[0:HG * TT, 0:P], ACT.Copy, scale=-1.0).then_inc(mneg_hi, 1)
                        act.wait_ge(bank_free[bank], off + turn + 1)
                        dst = q_ops[:, (item[1] + 1) % 2]
                        for part in (HI, LO):
                            act.dma_start(raw(dst[MAX_STRIP + part:MAX_STRIP + part + 1, :, :]).rearrange(
                                "a h (t p) -> a (h t) p", p=P), raw(mneg[:, part, :])).then_inc(m_sent, 16)
                    elif kind == "out":
                        t = item[1]
                        act.wait_ge(mv_ready, b * TT + t + 1)
                        act.activation(std[:, t % 2:t % 2 + 1], mv[:, t % 2, 1:2], ACT.Sqrt, bias=eps[:]
                                       ).then_inc(std_ready, 1)

            def drain(b, g, hh, k):
                act.wait_ge(pv_done, (b * GROUPS + g) * NE + k + 2)
                act.activation(y[:, g, hh * HALF:(hh + 1) * HALF], yb[:], ACT.Copy).then_inc(y_drained, 1)

            def exps(b, g, k, pair):
                c0 = steps[k][2]
                s = (b * GROUPS + g) * NE + k
                act.wait_ge(st_full, 2 * s + pair + 1)
                if pair == 0:
                    act.wait_ge(pv_done, s)
                act.activation(probs[:, slot_of(k, pair), :, c0:HALF], st[:, pair, :, c0:HALF], ACT.Exp,
                               scale=SCALE).then_inc(exp_done, 1)

            act.wait_ge(x_in, 16)
            for c in range(DC):
                act.activation(xs[:, HI, c, :], nat[:, c, :], ACT.Copy).then_inc(first_hi, 1)
            act.wait_ge(first_hi, DC)
            act.wait_ge(consts, N_CONSTS)
            act.activation(std[:, 0:1], eps[:], ACT.Copy).then_inc(exp_done, 2)
            run(0, lead=True)
            each_batch(act, run)

        @block.vector
        def _(dve):
            def run(b, lead=False):
                order, at, off = scope(b, lead)
                pieces = []
                for item in order:
                    kind = item[0]
                    if ends_half(item):
                        while pieces:
                            invert(b, *pieces.pop(0))
                        n = 2 * (b * GROUPS + item[1]) + steps[item[2]][0]
                        dve.wait_ge(pv_done, (b * GROUPS + item[1]) * NE + item[2] + 2)
                        dve.wait_ge(normed, n + 1)
                        dve.tensor_copy(den[:], db[:]).then_inc(den_drained, 1)
                        pieces = [(item[1], steps[item[2]][0], n) for n in range(DEN_PIECES)]
                        invert(b, *pieces.pop(0))
                    if not uses_bank(item):
                        continue
                    bank, turn = at[item]
                    src = shared[:, bank, :]
                    if pieces and (kind != "max" or item[2] % 2 == 0):
                        invert(b, *pieces.pop(0))
                    while pieces and kind == "out" and item[1] in (0, 2):
                        invert(b, *pieces.pop(0))
                    if kind == "proj":
                        g, i = item[1], item[2]
                        which, hh = i // 2, i % 2
                        n = 4 * (0 if lead else b * GROUPS + g + 1) + i
                        dve.wait_ge(hi_ready, n + 1)
                        gn = (g + 1) % GROUPS
                        bias = (keep["bq"], keep["bk"])[which]
                        cols = slice(hh * HALF, (hh + 1) * HALF)
                        dve.scalar_tensor_tensor(out=nat[:, 2 * which + LO, cols].bitcast(F32R), in0=src,
                                                 scalar=bias[:, gn:gn + 1], in1=nat[:, 2 * which + HI, cols],
                                                 op0=ALU.add, op1=ALU.subtract
                                                 ).then_inc(bank_free[bank], 1)
                    elif kind == "max":
                        h, slot, it, k0, n = maxes[item[2]]
                        dve.wait_ge(bank_full[bank], off + turn + 1)
                        dve.tensor_reduce(mx[:, h, slot:slot + 1], src[:, 0:n], AX.X, ALU.max
                                          ).then_inc(bank_free[bank], 1)
                    elif kind == "maxT":
                        n = 0 if lead else b * GROUPS + item[1] + 1
                        for k in range(2):
                            dve.wait_ge(bank_free[k], off + (turn if k == bank else turn_of_other(at[item])))
                        dve.tensor_copy(mrow[:, :, 0:4], mx[:, :, 0:4]).then_inc(mx_joined, 1)
                        dve.tensor_tensor(mrow[:, :, 4:8], mx[:, :, 4:8], mx[:, :, 8:12], ALU.max
                                          ).then_inc(mx_joined, 1)
                        dve.wait_ge(mneg_hi, n + 1)
                        dve.scalar_tensor_tensor(out=mneg[:, LO, :], in0=src[0:HG * TT, 0:P], scalar=-1.0,
                                                 in1=raw(mneg[:, HI, :]), op0=ALU.mult, op1=ALU.subtract
                                                 ).then_inc(bank_free[bank], 1)
                    elif kind == "out":
                        layer_norm(b, item[1], bank, off + turn, src)

            def turn_of_other(bank_turn):
                bank, turn = bank_turn
                return turn if bank == 0 else turn + 1

            def invert(b, g, hh, piece):
                n = 2 * (b * GROUPS + g) + hh
                width = HALF // DEN_PIECES
                cols = slice(piece * width, (piece + 1) * width)
                dve.wait_ge(den_drained, n + 1)
                dve.reciprocal(den[:, cols], den[:, cols]).then_inc(rden_ready, 1)

            def layer_norm(b, t, bank, turn, src):
                n = b * TT + t
                r = t % 2
                dve.wait_ge(bank_full[bank], turn + 1)
                dve.wait_ge(bo_added, n + 1)
                dve.wait_ge(x1_out[r], 16 * (b * (TT // 2) + t // 2))
                dve.tensor_tensor(x1[:, r], src, xres[:, r], ALU.add).then_inc(summed, 1)
                dve.wait_ge(summed, n + 1)
                dve.bn_stats(stats[:, t, :], x1[:, r]).then_inc(bank_free[bank], 1)
                plain(dve, bank_free[bank], turn + 1, dve_passed)
                dve.bn_aggr(mv[:, r, :], stats[:, t, :]).then_inc(mv_ready, 1)
                dve.wait_ge(std_ready, n + 1)
                dve.reciprocal(rstd[:, r:r + 1], std[:, r:r + 1]).then_inc(rstd_ready, 1)
                dve.wait_ge(rstd_ready, n + 1)
                dve.tensor_scalar(x1[:, r], x1[:, r], mv[:, r, 0:1], rstd[:, r:r + 1], ALU.subtract, ALU.mult
                                  ).then_inc(x1_ready, 1)

            for c in range(DC):
                dve.wait_ge(first_hi, c + 1)
                ins = dve.tensor_tensor(xs[:, LO, c, :], nat[:, c, :], raw(xs[:, HI, c, :]), ALU.subtract)
            ins.then_inc(x_split, 2)
            dve.memset(mrow[:], 0.0).then_inc(pv_done, 1)
            run(0, lead=True)
            each_batch(dve, run)


E_N = 16
F_N = 2048
FC = F_N // P
TABLE = D + E_N
QT = HALF // P
BLK = 4
NBLK = FC // BLK


def build_router(nc, x1_dram, w, table, logits_dram, logits, NB):
    with ExitStack() as ctx:
        sb = lambda name, shape, dt=F32: ctx.enter_context(nc.sbuf_tensor(name, shape, dt))
        ps = lambda name, shape, dt=F32: ctx.enter_context(nc.psum_tensor(name, shape, dt))
        sem = lambda name: ctx.enter_context(nc.semaphore(name))
        x1 = sb("r_x1", [P, 2, QT, D])
        xn = sb("r_xn", [P, 2, QT, D])
        xnT = sb("r_xnT", [P, 2, DC, HALF])
        square = sb("r_square", [P, 2, D])
        ss = sb("r_ss", [P, 2, QT])
        rms = sb("r_rms", [P, 2, QT])
        rinv = sb("r_rinv", [P, 2, QT])
        nw = sb("r_norm_weight", [P, D])
        rw = sb("r_weight", [P, DC, E_N])
        rb = sb("r_bias", [E_N, 1])
        eps = sb("r_eps", [P, 1])
        ident = sb("r_ident", [P, P])
        ps_t = ps("r_ps_t", [P, DC, HALF])
        ps_l = ps("r_ps_l", [E_N, 2, HALF])
        w_in, zeroed, consts = sem("r_w_in"), sem("r_zeroed"), sem("r_consts")
        x_in = [sem(f"r_x_in{u}") for u in range(2)]
        xn_out = [sem(f"r_xn_out{u}") for u in range(2)]
        ss_ready, rms_ready, rinv_ready, xn_ready = sem("ss_ready"), sem("rms_ready"), sem("rinv_ready"), sem("xn_ready")
        t_full = sem("t_full")
        act_copied, dve_copied = sem("act_copied"), sem("dve_copied")
        l_full, l_copied, l_out = sem("l_full"), sem("l_copied"), sem("l_out")
        block = ctx.enter_context(nc.Block())
        tokens = lambda dram, it, u: dram[bass.ds(it * T + u * HALF, HALF), :].rearrange("(t p) d -> p t d", p=P)

        has_next = lambda last, u: not (last and u == 1)

        def each(eng, run):
            if NB > 1:
                with eng.Fori(0, NB - 1) as it:
                    run(it, False)
            run(NB - 1, True)

        @block.sync
        def _(sp):
            sp.dma_start(nw[:], w["norm"].rearrange("(a n) -> a n", a=1).to_broadcast([P, D])).then_inc(w_in, 16)
            with nc.allow_non_contiguous_dma(reason="small router bias"):
                sp.dma_start(rb[:], w["rb"].rearrange("(e a) -> e a", a=1)).then_inc(w_in, 16)
            sp.dma_start(rw[:], w["rwT"].rearrange("(c p) e -> p c e", p=P)).then_inc(w_in, 16)

            def load(it, u):
                sp.dma_start(x1[:, u], tokens(x1_dram, it, u)).then_inc(x_in[u], 16)

            def run(it, last):
                for u in range(2):
                    sp.wait_ge(xn_ready, 2 * it + u + 1)
                    sp.dma_start(tokens(table, it, u)[:, :, 0:D], xn[:, u]).then_inc(xn_out[u], 16)
                    if not last:
                        load(it + 1, u)

            for u in range(2):
                load(0, u)
            each(sp, run)
            sp.wait_ge(l_copied, 2 * NB)
            sp.dma_start(logits_dram[:, :], logits[:]).then_inc(l_out, 16)
            sp.wait_ge(l_out, 16)
            for u in range(2):
                sp.wait_ge(xn_out[u], 16 * NB)

        @block.gpsimd
        def _(pool):
            pool.memset(eps[:], EPS).then_inc(consts, 1)
            pool.memset(ident[:], 0.0).then_inc(zeroed, 1)
            pool.wait_ge(zeroed, 1)
            pool.affine_select(out=ident[:], in_=ident[:], compare_op=ALU.not_equal, fill=1.0, base=0,
                               pattern=[[-1, P]], channel_multiplier=1).then_inc(consts, 1)

        @block.scalar
        def _(act):
            def squares(it, u):
                n = 2 * it + u
                act.wait_ge(x_in[u], 16 * (it + 1))
                if not (isinstance(n, int) and n == 0):
                    act.wait_ge(rinv_ready, n)
                for t in range(QT):
                    if t >= 2:
                        act.wait_ge(ss_ready, QT * n + t - 1)
                    act.activation(square[:, t % 2], x1[:, u, t, :], ACT.Square, accum_out=ss[:, u, t:t + 1]
                                   ).then_inc(ss_ready, 1)
                act.wait_ge(ss_ready, QT * n + QT)
                act.activation(rms[:, u], ss[:, u], ACT.Sqrt, bias=eps[:], scale=1.0 / D).then_inc(rms_ready, 1)

            def run(it, last):
                for u in range(2):
                    n = 2 * it + u
                    if has_next(last, u):
                        squares(it + u, 1 - u)
                    for c in range(0, DC, 2):
                        act.wait_ge(t_full, DC * n + c + 1)
                        act.wait_ge(l_full, 2 * it)
                        act.activation(xnT[:, u, c, :], ps_t[:, c, :], ACT.Copy).then_inc(act_copied, 1)

            act.wait_ge(consts, 2)
            squares(0, 0)
            each(act, run)

        @block.vector
        def _(dve):
            def normalise(it, u):
                m = 2 * it + u
                dve.wait_ge(rms_ready, m + 1)
                dve.reciprocal(rinv[:, u], rms[:, u]).then_inc(rinv_ready, 1)
                dve.wait_ge(rinv_ready, m + 1)
                dve.wait_ge(xn_out[u], 16 * it)
                if not (isinstance(m, int) and m == 0):
                    dve.wait_ge(t_full, DC * (m - 1))
                for t in range(QT):
                    ins = dve.scalar_tensor_tensor(out=xn[:, u, t, :], in0=x1[:, u, t, :],
                                                   scalar=rinv[:, u, t:t + 1], in1=nw[:],
                                                   op0=ALU.mult, op1=ALU.mult)
                ins.then_inc(xn_ready, 1)

            def store_logits(n, u):
                dve.wait_ge(l_full, n + 1)
                dve.tensor_scalar(logits[:, bass.ds(n * HALF, HALF)], ps_l[:, u, :], rb[:, 0:1], None, ALU.add
                                  ).then_inc(l_copied, 1)

            def run(it, last):
                for u in range(2):
                    n = 2 * it + u
                    if has_next(last, u):
                        normalise(it + u, 1 - u)
                    for c in range(1, DC, 2):
                        dve.wait_ge(t_full, DC * n + c + 1)
                        dve.wait_ge(l_full, 2 * it)
                        dve.tensor_copy(xnT[:, u, c, :], ps_t[:, c, :]).then_inc(dve_copied, 1)
                    if not (isinstance(n, int) and n == 0):
                        store_logits(n - 1, 1 - u)

            dve.wait_ge(w_in, 48)
            normalise(0, 0)
            run(0, NB == 1)
            if NB > 1:
                if NB > 2:
                    with dve.Fori(1, NB - 1) as it:
                        run(it, False)
                run(NB - 1, True)
            store_logits(2 * NB - 1, 1)

        @block.tensor
        def _(pe):
            def turn(it, u):
                n = 2 * it + u
                pe.wait_ge(xn_ready, n + 1)
                pe.wait_ge(act_copied, 2 * n)
                pe.wait_ge(dve_copied, 2 * n)
                for c in range(DC):
                    for t in range(QT):
                        mm = pe.transpose(ps_t[:, c, t * P:(t + 1) * P], xn[:, u, t, c * P:(c + 1) * P], ident[:])
                    mm.then_inc(t_full, 1)

            def run(it, last):
                for u in range(2):
                    n = 2 * it + u
                    if has_next(last, u):
                        turn(it + u, 1 - u)
                    pe.wait_ge(l_copied, 2 * it)
                    pe.wait_ge(act_copied, 2 * n + 2)
                    pe.wait_ge(dve_copied, 2 * n + 2)
                    for c in range(DC):
                        mm = pe.matmul(ps_l[:, u, :], rw[:, c, :], xnT[:, u, c, :], start=(c == 0), stop=(c == DC - 1))
                    mm.then_inc(l_full, 1)

            pe.wait_ge(consts, 2)
            pe.wait_ge(w_in, 48)
            turn(0, 0)
            each(pe, run)


def build_selection(nc, table, logits_dram, list_dram, logits, NB):
    N = NB * T
    CAP = N // E_N
    ROWS = E_N * NB
    NCH = N // P
    LO_N = 32
    HI_N = max(CAP // LO_N, 1)
    with ExitStack() as ctx:
        sb = lambda name, shape, dt=F32: ctx.enter_context(nc.sbuf_tensor(name, shape, dt))
        ps = lambda name, shape, dt=F32: ctx.enter_context(nc.psum_tensor(name, shape, dt))
        sem = lambda name: ctx.enter_context(nc.semaphore(name))
        ident = sb("s_ident", [P, P])
        same = sb("s_same_expert", [ROWS, E_N, NB])
        before = sb("s_earlier_sequence", [ROWS, E_N, NB])
        lg = sb("s_logits_tokens", [P, NCH, E_N])
        red = sb("s_red", [P, 3, NCH])
        x = sb("s_x", [ROWS, T])
        xs = sb("s_x_signed", [ROWS, T])
        junk = sb("s_junk", [ROWS, T])
        gt = sb("s_above", [ROWS, T])
        eq = sb("s_equal", [ROWS, T])
        ones = sb("s_ones", [ROWS, T])
        scan = sb("s_scan", [ROWS, T])
        sel = sb("s_selected", [ROWS, T])
        pos = sb("s_place", [ROWS, T])
        small = sb("s_small", [ROWS, 16])
        bits = sb("s_bits", [ROWS, 3], I32)
        counts = sb("s_counts", [ROWS, 3])
        thr = sb("s_threshold", [ROWS, 1], I32)
        cand = sb("s_candidates", [ROWS, 3], I32)
        keep = sb("s_keep", [ROWS, 3])
        place = sb("s_place_tokens", [P, TT, E_N, NB], I32)
        row = sb("s_list_row", [P, TT, E_N, NB], I32)
        col = sb("s_list_col", [P, TT, E_N, NB], I32)
        iota_i = sb("s_iota_i", [P, LO_N], I32)
        iota = sb("s_iota", [P, LO_N], F32)
        cid_i = sb("s_chunk_i", [P, TT, NB], I32)
        cid = sb("s_chunk", [P, TT, NB], BF16)
        pid_i = sb("s_partition_i", [P, 1], I32)
        pid = sb("s_partition", [P, 1])
        oh_row = sb("s_row_onehot", [P, 2, TT, NB, HI_N], BF16)
        oh_tok = sb("s_row_tokens", [P, 2, TT, NB, 2, HI_N], BF16)
        oh_col = sb("s_col_onehot", [P, 2, TT, NB, LO_N], BF16)
        join = sb("s_join", [2 * HI_N, HI_N])
        parts = sb("s_list_parts", [2 * HI_N, 2, LO_N])
        lists = sb("s_list", [HI_N, 2, LO_N], U32)
        ps_lg = ps("s_ps_lg", [P, NCH, E_N])
        ps_pos = ps("s_ps_pos", [P, TT, ROWS])
        ps_cnt = ps("s_ps_cnt", [ROWS, 16])
        ps_join = ps("s_ps_join", [HI_N, HALF])
        ps_list = ps("s_ps_list", [2 * HI_N, 2, HALF])
        consts, made, x_in, lg_full = sem("s_consts"), sem("s_made"), sem("s_x_in"), sem("s_lg_full")
        d = sem("s_dve_step")
        shifted, exped, probs_ready, probs_out = sem("s_shifted"), sem("s_exped"), sem("s_probs_ready"), sem("s_probs_out")
        passed = sem("s_passed")
        counted, grouped = sem("s_counted"), sem("s_grouped")
        tallied, offset = sem("s_tallied"), sem("s_offset")
        pos_ready, pos_turned, rows_ready, row_pids, onehots, list_mm, list_ready, list_copied, joined = (
            sem("s_pos_ready"), sem("s_pos_turned"), sem("s_rows_ready"), sem("s_row_pids"), sem("s_onehots"),
            sem("s_list_mm"), sem("s_list_ready"), sem("s_list_copied"), sem("s_joined"))
        join_zero, pid_ready, pe_passed = sem("s_join_zero"), sem("s_pid_ready"), sem("s_pe_passed")
        list_out = [sem(f"s_list_out{r}") for r in range(2)]
        block = ctx.enter_context(nc.Block())
        e_before = lambda it, r: not (isinstance(it, int) and it == 0)
        has_before = lambda it, r: r == 1 or e_before(it, r)

        def await_twin(eng, semaphore, it, r):
            if e_before(it, r):
                eng.wait_ge(semaphore, 2 * it + r - 1)

        def each(eng, run):
            run(0, False)
            with eng.Fori(1, E_N // 2) as it:
                run(it, False)

        join_bank = (ps_pos[0:HI_N, 0, 0:LO_N], ps_join[:, 0:LO_N])

        BITS = 31
        SEARCHES = 1 + (BITS - 1) // 2

        @block.sync
        def _(sp):
            sp.dma_start(x[:], logits_dram.rearrange("e (s t) -> (e s) t", t=T)).then_inc(x_in, 16)
            sp.wait_ge(probs_ready, 1)
            sp.dma_start(table.rearrange("(c p) k -> p c k", p=P)[:, :, D:TABLE], lg[:]).then_inc(probs_out, 16)
            with sp.Fori(0, E_N // 2) as it:
                for r in range(2):
                    e = 2 * it + r
                    sp.wait_ge(list_ready, e + 1)
                    sp.dma_start(list_dram[bass.ds(e, 1), :].rearrange("a (h l) -> (a h) l", l=LO_N), lists[:, r, :]
                                 ).then_inc(list_out[r], 16)
            sp.wait_ge(probs_out, 16)
            for r in range(2):
                sp.wait_ge(list_out[r], 16 * E_N // 2)

        @block.gpsimd
        def _(pool):
            pool.memset(ident[:], 0.0).then_inc(made, 1)
            pool.memset(same[:], 1.0).then_inc(made, 1)
            pool.iota(iota_i[:], pattern=[[1, LO_N]], base=0, channel_multiplier=0).then_inc(made, 1)
            pool.iota(cid_i[:], pattern=[[1, TT], [TT, NB]], base=0, channel_multiplier=0).then_inc(made, 1)
            pool.iota(pid_i[:], pattern=[[0, 1]], base=0, channel_multiplier=1).then_inc(made, 1)
            pool.wait_ge(made, 5)
            pool.affine_select(out=ident[:], in_=ident[:], compare_op=ALU.not_equal, fill=1.0, base=0,
                               pattern=[[-1, P]], channel_multiplier=1).then_inc(consts, 1)
            pool.affine_select(out=same[:], in_=same[:], compare_op=ALU.is_ge, fill=0.0, base=0,
                               pattern=[[-NB, E_N], [0, NB]], channel_multiplier=1).then_inc(made, 1)
            pool.wait_ge(made, 6)
            pool.affine_select(out=same[:], in_=same[:], compare_op=ALU.is_ge, fill=0.0, base=NB - 1,
                               pattern=[[NB, E_N], [0, NB]], channel_multiplier=-1).then_inc(made, 1)
            pool.wait_ge(made, 7)
            pool.affine_select(out=before[:], in_=same[:], compare_op=ALU.is_gt, fill=0.0, base=0,
                               pattern=[[NB, E_N], [1, NB]], channel_multiplier=-1).then_inc(consts, 1)
            pool.memset(join[:], 0.0).then_inc(join_zero, 1)
            pool.wait_ge(join_zero, 1)
            pool.affine_select(out=join[:], in_=join[:], compare_op=ALU.not_equal, fill=1.0, base=0,
                               pattern=[[-1, HI_N]], channel_multiplier=1).then_inc(join_zero, 1)
            pool.wait_ge(join_zero, 2)
            pool.affine_select(out=join[:], in_=join[:], compare_op=ALU.not_equal, fill=float(P), base=-HI_N,
                               pattern=[[-1, HI_N]], channel_multiplier=1).then_inc(consts, 1)

        @block.scalar
        def _(act):
            act.wait_ge(shifted, 1)
            act.activation(lg[:], lg[:], ACT.Exp).then_inc(exped, 1)
            act.wait_ge(pid_ready, 1)

            def copy_list(it, r):
                act.wait_ge(list_mm, 2 * it + r + 1)
                await_twin(act, joined, it, r)
                act.activation(parts[:, r], ps_list[:, r, 0:LO_N], ACT.Copy).then_inc(list_copied, 1)

            def run(it, last):
                for r in range(2):
                    act.wait_ge(rows_ready, 2 * it + r + 1)
                    await_twin(act, list_mm, it, r)
                    act.activation(oh_tok[:, r, :, :, 0, :], oh_row[:, r], ACT.Copy, scale=pid[:, 0:1]
                                   ).then_inc(row_pids, 1)
                    if has_before(it, r):
                        copy_list(it - 1 + r, 1 - r)

            each(act, run)
            copy_list(E_N // 2 - 1, 1)

        @block.tensor
        def _(pe):
            pe.wait_ge(consts, 2)
            for c in range(NCH):
                mm = pe.transpose(ps_lg[:, c, :], logits[:, c * P:(c + 1) * P], ident[0:E_N, 0:E_N])
            mm.then_inc(lg_full, 1)
            group = same[:].rearrange("k e s -> k (e s)")
            pe.wait_ge(counted, 1)
            pe.matmul(ps_cnt[:, 0:1], group, small[:, 0:1], start=True, stop=True).then_inc(grouped, 1)
            with pe.Fori(0, SEARCHES) as i:
                pe.wait_ge(counted, i + 2)
                pe.matmul(ps_cnt[:, 5:8], group, counts[:], start=True, stop=True).then_inc(grouped, 1)
            pe.wait_ge(tallied, 1)
            pe.matmul(ps_cnt[:, 2:3], group, small[:, 5:6], start=True, stop=True)
            pe.matmul(ps_cnt[:, 3:4], before[:].rearrange("k e s -> k (e s)"), scan[:, T - 1:T], start=True, stop=True
                      ).then_inc(offset, 1)
            pe.wait_ge(tallied, 2)
            pe.matmul(ps_cnt[:, 4:5], before[:].rearrange("k e s -> k (e s)"), scan[:, T - 1:T], start=True, stop=True
                      ).then_inc(offset, 1)
            pe.wait_ge(consts, 3)
            pe.wait_ge(pos_ready, 1)
            for b in range(TT):
                mm = pe.transpose(ps_pos[:, b, :], pos[:, b * P:(b + 1) * P], ident[0:ROWS, 0:ROWS])
            mm.then_inc(pos_turned, 1)

            def join_list(it, r):
                await_twin(pe, list_ready, it, r)
                plain(pe, list_copied, 2 * it + r + 1, pe_passed)
                pe.matmul(join_bank[r], join[:], parts[:, r, :],
                          start=True, stop=True).then_inc(joined, 1)

            def run(it, last):
                for r in range(2):
                    e = 2 * it + r
                    await_twin(pe, list_copied, it, r)
                    pe.wait_ge(row_pids, e + 1)
                    pe.wait_ge(onehots, e + 1)
                    for n in range(NCH):
                        b, s = n // NB, n % NB
                        mm = pe.matmul(ps_list[:, r, 0:LO_N], oh_tok[:, r, b, s].rearrange("p a h -> p (a h)"),
                                       oh_col[:, r, b, s, :], start=(n == 0), stop=(n == NCH - 1))
                    mm.then_inc(list_mm, 1)
                    if has_before(it, r):
                        join_list(it - 1 + r, 1 - r)

            each(pe, run)
            join_list(E_N // 2 - 1, 1)

        @block.vector
        def _(dve):
            step = [0]

            def then(ins):
                step[0] += 1
                ins.then_inc(d, 1)
                dve.wait_ge(d, step[0])

            dve.wait_ge(lg_full, 1)
            then(dve.tensor_reduce(red[:, 0, :], ps_lg[:], AX.X, ALU.max))
            dve.tensor_tensor(lg[:], ps_lg[:], red[:, 0, :].unsqueeze(2).to_broadcast([P, NCH, E_N]), ALU.subtract
                              ).then_inc(shifted, 1)
            dve.wait_ge(x_in, 16)
            then(dve.tensor_scalar(junk[:], x[:], 0.0, None, ALU.is_ge, ALU.add, accum_out=small[:, 0:1]))
            dve.memset(ones[:], 1.0).then_inc(counted, 1)
            dve.wait_ge(exped, 1)
            then(dve.tensor_reduce(red[:, 1, :], lg[:], AX.X, ALU.add))
            then(dve.reciprocal(red[:, 2, :], red[:, 1, :]))
            dve.tensor_tensor(lg[:], lg[:], red[:, 2, :].unsqueeze(2).to_broadcast([P, NCH, E_N]), ALU.mult
                              ).then_inc(probs_ready, 1)
            dve.wait_ge(grouped, 1)
            then(dve.tensor_scalar(small[:, 1:2], ps_cnt[:, 0:1], float(CAP), None, ALU.is_ge))
            then(dve.tensor_scalar(small[:, 2:3], small[:, 1:2], 2.0, -1.0, ALU.mult, ALU.add))
            then(dve.tensor_scalar(small[:, 3:4], small[:, 1:2], float(2 * CAP - N - 1), float(N - CAP + 1),
                                   ALU.mult, ALU.add))
            then(dve.tensor_scalar(xs[:], x[:], small[:, 2:3], None, ALU.mult))
            then(dve.memset(thr[:], 0))
            then(dve.memset(bits[:], 1 << (BITS - 1)))

            def search(i, done):
                dve.tensor_tensor(cand[:], thr[:].to_broadcast([ROWS, 3]), bits[:], ALU.bitwise_or).then_inc(d, 1)
                dve.wait_ge(d, done + 1)
                for j, mark in enumerate((junk, gt, eq)):
                    ins = dve.tensor_scalar(mark[:], xs[:], cand[:, j:j + 1].bitcast(F32), None, ALU.is_ge, ALU.add,
                                            accum_out=counts[:, j:j + 1])
                ins.then_inc(counted, 1)
                dve.tensor_scalar(bits[:], bits[:], 2, None, ALU.logical_shift_right).then_inc(d, 1)
                dve.wait_ge(grouped, i + 2)
                dve.wait_ge(d, done + 2)
                dve.tensor_tensor(keep[:], ps_cnt[:, 5:8], small[:, 3:4].to_broadcast([ROWS, 3]), ALU.is_ge
                                  ).then_inc(d, 1)
                for j in range(3):
                    plain(dve, d, done + 3 + j, passed)
                    dve.copy_predicated(thr[:], keep[:, j:j + 1].bitcast(U32), cand[:, j:j + 1]).then_inc(d, 1)
                dve.wait_ge(d, done + 6)

            PER = 6
            search(0, step[0])
            step[0] += PER
            for j in range(3):
                then(dve.memset(bits[:, j:j + 1], (j + 1) << (BITS - 3)))
            first = step[0] - PER
            with dve.Fori(1, SEARCHES) as i:
                search(i, i * PER + first)
            step[0] = first + SEARCHES * PER
            then(dve.tensor_scalar(small[:, 7:8], thr[:].bitcast(F32), small[:, 2:3], None, ALU.mult))
            then(dve.tensor_scalar(gt[:], x[:], small[:, 7:8], None, ALU.is_gt, ALU.add, accum_out=small[:, 5:6]))
            then(dve.tensor_scalar(eq[:], x[:], small[:, 7:8], None, ALU.is_equal))
            dve.tensor_tensor_scan(scan[:], ones[:], eq[:], 0.0, ALU.mult, ALU.add).then_inc(tallied, 1)
            dve.wait_ge(offset, 1)
            then(dve.tensor_scalar(small[:, 8:9], ps_cnt[:, 2:3], -1.0, float(CAP), ALU.mult, ALU.add))
            then(dve.tensor_tensor(small[:, 9:10], small[:, 8:9], ps_cnt[:, 3:4], ALU.subtract))
            then(dve.scalar_tensor_tensor(out=sel[:], in0=scan[:], scalar=small[:, 9:10], in1=eq[:],
                                          op0=ALU.is_le, op1=ALU.mult))
            then(dve.tensor_tensor(sel[:], sel[:], gt[:], ALU.add))
            dve.tensor_tensor_scan(scan[:], ones[:], sel[:], 0.0, ALU.mult, ALU.add).then_inc(tallied, 1)
            dve.wait_ge(offset, 2)
            then(dve.tensor_copy(small[:, 10:11], ps_cnt[:, 4:5]))
            dve.scalar_tensor_tensor(out=pos[:], in0=scan[:], scalar=small[:, 10:11], in1=sel[:],
                                     op0=ALU.add, op1=ALU.mult).then_inc(pos_ready, 1)
            then(dve.tensor_copy(iota[:], iota_i[:]))
            then(dve.tensor_copy(cid[:], cid_i[:]))
            then(dve.tensor_copy(pid[:], pid_i[:]))
            dve.wait_ge(pos_turned, 1)
            then(dve.tensor_scalar(place[:].rearrange("p b e s -> p b (e s)"), ps_pos[:], -1.0, None, ALU.add))
            then(dve.tensor_scalar(row[:], place[:], 5, None, ALU.arith_shift_right))
            then(dve.tensor_scalar(col[:], place[:], LO_N - 1, None, ALU.bitwise_and))
            dve.memset(small[:, 11:12], 0.0).then_inc(pid_ready, 1)

            def write_list(it, r):
                dve.wait_ge(joined, 2 * it + r + 1)
                dve.wait_ge(list_out[r], 16 * it)
                dve.tensor_copy(lists[:, r], join_bank[r]).then_inc(list_ready, 1)

            def run(it, last):
                for r in range(2):
                    e = 2 * it + r
                    await_twin(dve, list_mm, it, r)
                    dve.tensor_tensor(
                        oh_row[:, r], row[:, :, bass.ds(e, 1), :].rearrange("p b a s -> p b (a s)").unsqueeze(3)
                        .to_broadcast([P, TT, NB, HI_N]),
                        iota[:, 0:HI_N].unsqueeze(1).unsqueeze(1).to_broadcast([P, TT, NB, HI_N]), ALU.is_equal
                    ).then_inc(rows_ready, 1)
                    dve.tensor_tensor(
                        oh_col[:, r], col[:, :, bass.ds(e, 1), :].rearrange("p b a s -> p b (a s)").unsqueeze(3)
                        .to_broadcast([P, TT, NB, LO_N]),
                        iota[:].unsqueeze(1).unsqueeze(1).to_broadcast([P, TT, NB, LO_N]), ALU.is_equal)
                    dve.wait_ge(rows_ready, e + 1)
                    dve.tensor_tensor(oh_tok[:, r, :, :, 1, :], oh_row[:, r],
                                      cid[:].unsqueeze(3).to_broadcast([P, TT, NB, HI_N]), ALU.mult
                                      ).then_inc(onehots, 1)
                    if e_before(it, r):
                        write_list(it - 1, r)

            each(dve, run)
            for r in range(2):
                write_list(E_N // 2 - 1, r)


def build_experts(nc, w, table, list_dram, acc_dram, NB):
    N = NB * T
    CAP = N // E_N
    CT = CAP // P
    with ExitStack() as ctx:
        sb = lambda name, shape, dt=F32: ctx.enter_context(nc.sbuf_tensor(name, shape, dt))
        ps = lambda name, shape, dt=F32: ctx.enter_context(nc.psum_tensor(name, shape, dt))
        sem = lambda name: ctx.enter_context(nc.semaphore(name))
        idx = sb("m_idx", [P, 2, CT], U32)
        xg = sb("m_rows", [P, 2, CT, TABLE])
        xe = sb("m_tokens_t", [P, 2, 2, DC, CAP], F32R)
        w1 = sb("m_w1_raw", [P, 2, DC, BLK * P])
        w2 = sb("m_w2_raw", [P, 2, BLK, D])
        w1s = sb("m_w1_parts", [P, 2, 2, DC, BLK * P], F32R)
        w2s = sb("m_w2_parts", [P, 2, 2, BLK, D], F32R)
        h = sb("m_hidden", [P, 2, CAP])
        hs = sb("m_hidden_parts", [P, 2, 2, CAP], F32R)
        b1 = sb("m_b1", [P, 2, FC])
        b2 = sb("m_b2", [P, 2, D])
        gates = sb("m_gates", [P, 2, CT])
        out = sb("m_out", [P, CT, ACC])
        ident = sb("m_ident", [P, P])
        ps_t = ps("m_ps_t", [P, 2, HALF])
        ps_h = ps("m_ps_h", [P, 2, HALF])
        ps_y = ps("m_ps_y", [P, CT, HALF])

        idx_in = [sem(f"idx_in{r}") for r in range(2)]
        gathered = [sem(f"gathered{r}") for r in range(2)]
        w1_in = [sem(f"w1_in{r}") for r in range(2)]
        w2_in = [sem(f"w2_in{r}") for r in range(2)]
        b_in = [sem(f"b_in{r}") for r in range(2)]
        passed = sem("m_passed")
        w_hi, w_lo = sem("w_hi"), sem("w_lo")
        t_full, xe_hi, xe_lo, gate_ready = sem("m_t_full"), sem("xe_hi"), sem("xe_lo"), sem("gate_ready")
        h_full, gelu_done, h_hi, h_lo, fc2_done = sem("h_full"), sem("gelu_done"), sem("h_hi"), sem("h_lo"), sem("fc2_done")
        y_copied, out_ready, scattered, consts, zeroed = (sem("y_copied"), sem("out_ready"), sem("scattered"),
                                                          sem("m_consts"), sem("m_zeroed"))
        block = ctx.enter_context(nc.Block())

        def each_pair(eng, run):
            with eng.Fori(0, E_N // 2 - 1) as it:
                run(it, False)
            run(E_N // 2 - 1, True)

        def has_next(last, r):
            return not (last and r == 1)

        TURN_AT = {6: (0, 1), 9: (2, 3)}

        PIECES = 4

        @block.sync
        def _(sp):
            def load_block(e, e_slot_free, blk):
                q = blk % 2
                if e_slot_free is not None:
                    sp.wait_ge(w_lo, e_slot_free)
                sp.dma_start(w1[:, q], w["w1T"][bass.ds(e, 1)].rearrange("a (c p) f -> p (a c) f", p=P)
                             [:, :, blk * BLK * P:(blk + 1) * BLK * P]).then_inc(w1_in[q], 16)
                sp.dma_start(w2[:, q], w["w2T"][bass.ds(e, 1), blk * BLK * P:(blk + 1) * BLK * P, :].rearrange(
                    "a (f p) n -> p (a f) n", p=P)).then_inc(w2_in[q], 16)

            def load_small(e, r):
                sp.dma_start(idx[:, r, :], list_dram[bass.ds(e, 1), :].rearrange("a (p j) -> p (a j)", j=CT)
                             ).then_inc(idx_in[r], 16)
                sp.dma_start(b1[:, r, :], w["b1T"][bass.ds(e, 1)].rearrange("a p f -> p (a f)")).then_inc(b_in[r], 16)
                sp.dma_start(b2[:, r, :], w["b2"][bass.ds(e, 1), :].to_broadcast([P, D])).then_inc(b_in[r], 16)

            load_small(0, 0)
            load_block(0, None, 0)
            load_block(0, None, 1)

            def run(it, last):
                for r in range(2):
                    e = 2 * it + r
                    for blk in range(NBLK):
                        if blk == 1 and has_next(last, r):
                            sp.wait_ge(scattered, 16 * CT * e)
                            load_small(e + 1, 1 - r)
                        nb = blk + 2
                        if nb < NBLK:
                            load_block(e, PIECES * (e * NBLK + blk + 1), nb)
                        elif has_next(last, r):
                            load_block(e + 1, PIECES * (e * NBLK + blk + 1), nb - NBLK)

            each_pair(sp, run)

        @block.gpsimd
        def _(pool):
            pool.memset(out[:], 0.0).then_inc(consts, 1)
            pool.memset(ident[:], 0.0).then_inc(zeroed, 1)
            pool.wait_ge(zeroed, 1)
            pool.affine_select(out=ident[:], in_=ident[:], compare_op=ALU.not_equal, fill=1.0, base=0,
                               pattern=[[-1, P]], channel_multiplier=1).then_inc(consts, 1)

            def gather(e, r, count):
                plain(pool, idx_in[r], 16 * count, passed)
                for j in range(CT):
                    pool.indirect_dma_start(out=xg[:, r, j, :], out_offset=None, in_=table[:, :],
                                            in_offset=bass.IndirectOffsetOnAxis(ap=idx[:, r, j:j + 1], axis=0)
                                            ).then_inc(gathered[r], 16)

            def run(it, last):
                for r in range(2):
                    e = 2 * it + r
                    if has_next(last, r):
                        pool.wait_ge(xe_lo, DC * e + 1)
                        pool.wait_ge(gate_ready, e)
                        gather(e + 1, 1 - r, it + r + 1)
                    pool.wait_ge(scattered, 16 * CT * e)
                    for j in range(CT):
                        plain(pool, out_ready, CT * e + j + 1, passed)
                        pool.indirect_dma_start(out=acc_dram[:, :], out_offset=bass.IndirectOffsetOnAxis(
                            ap=idx[:, r, j:j + 1], axis=0), in_=out[:, j, :], in_offset=None,
                            compute_op=ALU.add).then_inc(scattered, 16)

            gather(0, 0, 1)
            each_pair(pool, run)
            pool.wait_ge(scattered, 16 * CT * E_N)

        @block.scalar
        def _(act):
            def split_hi(B, q, piece):
                n = 2 * (piece % 2)
                if piece < 2:
                    act.activation(w1s[:, q, HI, n:n + 2, :], w1[:, q, n:n + 2, :], ACT.Copy).then_inc(w_hi, 1)
                else:
                    act.activation(w2s[:, q, HI, n:n + 2, :], w2[:, q, n:n + 2, :], ACT.Copy).then_inc(w_hi, 1)

            def token_hi(r, c, cc):
                act.wait_ge(t_full, cc + 1)
                act.activation(xe[:, r, HI, c, :], ps_t[:, c % 2, 0:CAP], ACT.Copy).then_inc(xe_hi, 1)

            act.wait_ge(consts, 2)
            act.activation(gates[:, 0, :], ident[:, 0:CT], ACT.Copy).then_inc(gelu_done, 2)
            act.wait_ge(w1_in[0], 16)
            act.wait_ge(w2_in[0], 16)
            for piece in range(PIECES):
                split_hi(0, 0, piece)
            for c in range(DC):
                token_hi(0, c, c)

            def run(it, last):
                for r in range(2):
                    e = 2 * it + r
                    act.wait_ge(b_in[r], 32 * (it + 1))
                    for f in range(FC):
                        k = e * FC + f
                        blk = f // BLK
                        act.wait_ge(h_full, k + 1)
                        act.wait_ge(h_lo, k)
                        act.activation(h[:, f % 2, :], ps_h[:, f % 2, 0:CAP], ACT.Gelu, bias=b1[:, r, f:f + 1]
                                       ).then_inc(gelu_done, 1)
                        if blk < NBLK - 1 or has_next(last, r):
                            B, q = e * NBLK + blk + 1, (blk + 1) % 2
                            if f % BLK == 0:
                                use = (it * 2 + r) * (NBLK // 2) + (blk + 1) // 2
                                act.wait_ge(w1_in[q], 16 * (use + 1))
                                act.wait_ge(w2_in[q], 16 * (use + 1))
                                act.wait_ge(fc2_done, BLK * (B - 1) + 1)
                            split_hi(B, q, f % BLK)
                        if has_next(last, r) and f in TURN_AT:
                            for c in TURN_AT[f]:
                                token_hi(1 - r, c, DC * (e + 1) + c)

            each_pair(act, run)

        @block.vector
        def _(dve):
            def split_lo(q, piece, n_done):
                dve.wait_ge(w_hi, n_done + 1)
                n = 2 * (piece % 2)
                if piece < 2:
                    dve.tensor_tensor(w1s[:, q, LO, n:n + 2, :], w1[:, q, n:n + 2, :], raw(w1s[:, q, HI, n:n + 2, :]),
                                      ALU.subtract).then_inc(w_lo, 1)
                else:
                    dve.tensor_tensor(w2s[:, q, LO, n:n + 2, :], w2[:, q, n:n + 2, :], raw(w2s[:, q, HI, n:n + 2, :]),
                                      ALU.subtract).then_inc(w_lo, 1)

            def token_lo(r, c, cc):
                dve.wait_ge(xe_hi, cc + 1)
                dve.tensor_tensor(xe[:, r, LO, c, :], ps_t[:, c % 2, 0:CAP], raw(xe[:, r, HI, c, :]), ALU.subtract
                                  ).then_inc(xe_lo, 1)

            def read_gates(e, r, count):
                dve.wait_ge(gathered[r], 16 * CT * count)
                dve.tensor_copy(gates[:, r, :], xg[:, r, :, bass.ds(e + D, 1)].rearrange("p j a -> p (j a)")
                                ).then_inc(gate_ready, 1)

            dve.wait_ge(gelu_done, 2)
            dve.memset(h[:], 0.0).then_inc(h_lo, 1)
            dve.memset(gates[:], 0.0).then_inc(xe_lo, 1)
            for piece in range(PIECES):
                split_lo(0, piece, piece)
            for c in range(DC):
                token_lo(0, c, c)
            read_gates(0, 0, 1)

            def run(it, last):
                for r in range(2):
                    e = 2 * it + r
                    for f in range(FC):
                        k = e * FC + f
                        blk = f // BLK
                        dve.wait_ge(gelu_done, k + 3)
                        dve.wait_ge(fc2_done, k)
                        dve.tensor_copy(hs[:, f % 2, HI, :], h[:, f % 2, :]).then_inc(h_hi, 1)
                        dve.wait_ge(h_hi, k + 1)
                        dve.tensor_tensor(hs[:, f % 2, LO, :], h[:, f % 2, :], raw(hs[:, f % 2, HI, :]), ALU.subtract
                                          ).then_inc(h_lo, 1)
                        if blk < NBLK - 1 or has_next(last, r):
                            split_lo((blk + 1) % 2, f % BLK, (e * NBLK + blk + 1) * PIECES + f % BLK)
                        if has_next(last, r) and f in TURN_AT:
                            for c in TURN_AT[f]:
                                token_lo(1 - r, c, DC * (e + 1) + c)
                            if f == max(TURN_AT):
                                read_gates(e + 1, 1 - r, it + r + 1)
                    dve.wait_ge(fc2_done, FC * (e + 1) + 1)
                    dve.wait_ge(scattered, 16 * CT * e)
                    dve.wait_ge(gate_ready, e + 1)
                    for j in range(CT):
                        dve.tensor_tensor(out[:, j, 0:D], ps_y[:, j, :], b2[:, r, :], ALU.add).then_inc(y_copied, 1)
                    for j in range(CT):
                        dve.wait_ge(y_copied, CT * e + j + 1)
                        dve.tensor_copy(out[:, j, D:D + 1], gates[:, r, j:j + 1])
                        dve.tensor_scalar(out[:, j, 0:D], out[:, j, 0:D], gates[:, r, j:j + 1], None, ALU.mult
                                          ).then_inc(out_ready, 1)

            each_pair(dve, run)

        @block.tensor
        def _(pe):
            def turn(r, c, cc):
                pe.wait_ge(xe_lo, cc)
                for j in range(CT):
                    mm = pe.transpose(ps_t[:, c % 2, j * P:(j + 1) * P], xg[:, r, j, c * P:(c + 1) * P], ident[:])
                mm.then_inc(t_full, 1)

            def product(bank, pairs, first, final):
                for n, (a, b) in enumerate(pairs):
                    mm = pe.matmul(bank, a, b, start=(first and n == 0), stop=(final and n == len(pairs) - 1))
                return mm

            THREE = ((HI, HI), (LO, HI), (HI, LO))

            def fc1(e, r, f):
                k = e * FC + f
                blk, q = f // BLK, (f // BLK) % 2
                cols = slice((f % BLK) * P, (f % BLK + 1) * P)
                if f == 0:
                    pe.wait_ge(xe_lo, DC * (e + 1) + 1)
                if f % BLK == 0:
                    pe.wait_ge(w_lo, PIECES * (e * NBLK + blk) + 2)
                pe.wait_ge(gelu_done, k + 1)
                product(ps_h[:, f % 2, 0:CAP],
                        [(w1s[:, q, a, c, cols], xe[:, r, b, c, :]) for a, b in THREE for c in range(DC)],
                        True, True).then_inc(h_full, 1)

            def fc2(e, r, f):
                k = e * FC + f
                blk, q = f // BLK, (f // BLK) % 2
                if f == 0:
                    pe.wait_ge(y_copied, CT * e)
                if f % BLK == 0:
                    pe.wait_ge(w_lo, PIECES * (e * NBLK + blk) + 4)
                pe.wait_ge(h_lo, k + 2)
                for j in range(CT):
                    mm = product(ps_y[:, j, :],
                                 [(hs[:, f % 2, a, j * P:(j + 1) * P], w2s[:, q, b, f % BLK, :]) for a, b in THREE],
                                 f == 0, f == FC - 1)
                mm.then_inc(fc2_done, 1)

            pe.wait_ge(consts, 2)
            pe.wait_ge(gathered[0], 16 * CT)
            for c in range(DC):
                if c == 0:
                    pe.transpose(ps_t[:, 0, 0:P], ident[:], ident[:]).then_inc(fc2_done, 1)
                turn(0, c, c)

            def run(it, last):
                for r in range(2):
                    e = 2 * it + r
                    for f in range(FC):
                        fc1(e, r, f)
                        if f > 0:
                            fc2(e, r, f - 1)
                        if has_next(last, r) and f in TURN_AT:
                            if f == min(TURN_AT):
                                pe.wait_ge(gathered[1 - r], 16 * CT * (it + r + 1))
                            for c in TURN_AT[f]:
                                turn(1 - r, c, DC * (e + 1) + c)
                    fc2(e, r, FC - 1)

            each_pair(pe, run)


def build_final(nc, x1_dram, acc_dram, out_dram, NB):
    BUFS = 4
    ROUNDS = NB * T // (BUFS * HALF)
    assert ROUNDS * BUFS * HALF == NB * T
    with ExitStack() as ctx:
        sb = lambda name, shape, dt=F32: ctx.enter_context(nc.sbuf_tensor(name, shape, dt))
        sem = lambda name: ctx.enter_context(nc.semaphore(name))
        acc = sb("f_acc", [P, BUFS, QT, ACC])
        z = sb("f_z", [P, BUFS, QT, D])
        sums = sb("f_sums", [P, 4, QT])
        stats = sb("f_stats", [P, QT, 6])
        mv = sb("f_mv", [P, BUFS, QT, 2])
        std = sb("f_std", [P, BUFS, QT])
        rstd = sb("f_rstd", [P, BUFS, QT])
        shift = sb("f_shift", [P, BUFS, QT])
        eps = sb("f_eps", [P, 1])
        passed = sem("f_passed")
        a_in = [sem(f"f_in{u}") for u in range(BUFS)]
        z_out = [sem(f"f_out{u}") for u in range(BUFS)]
        consts, d, mv_ready, std_ready, rstd_ready, shift_ready, z_ready = (
            sem("f_consts"), sem("f_dve_step"), sem("f_mv_ready"), sem("f_std_ready"), sem("f_rstd_ready"),
            sem("f_shift_ready"), sem("f_z_ready"))
        block = ctx.enter_context(nc.Block())
        tokens = lambda dram, it, u: dram[bass.ds((it * BUFS + u) * HALF, HALF), :].rearrange("(t p) d -> p t d", p=P)

        @block.sync
        def _(sp):
            def load(it, u):
                sp.dma_start(acc[:, u], tokens(acc_dram, it, u)).then_inc(a_in[u], 16)
                sp.dma_start(z[:, u], tokens(x1_dram, it, u)).then_inc(a_in[u], 16)

            for u in range(BUFS):
                load(0, u)
            if ROUNDS > 1:
                with sp.Fori(1, ROUNDS) as it:
                    for u in range(BUFS):
                        sp.wait_ge(z_out[u], 16 * it)
                        load(it, u)
            for u in range(BUFS):
                sp.wait_ge(z_out[u], 16 * ROUNDS)

        @block.gpsimd
        def _(pool):
            pool.memset(eps[:], EPS).then_inc(consts, 1)

        @block.scalar
        def _(act):
            def finish(it, u):
                n = it * BUFS + u
                act.wait_ge(shift_ready, n + 1)
                for t in range(QT):
                    ins = act.activation(z[:, u, t, :], z[:, u, t, :], ACT.Identity, scale=rstd[:, u, t:t + 1],
                                         bias=shift[:, u, t:t + 1])
                ins.then_inc(z_ready, 1)
                act.wait_ge(z_ready, n + 1)
                act.dma_start(tokens(out_dram, it, u), z[:, u]).then_inc(z_out[u], 16)

            def run(it):
                for u in range(BUFS):
                    if u > 0:
                        finish(it, u - 1)
                    elif not isinstance(it, int):
                        finish(it - 1, BUFS - 1)
                    act.wait_ge(mv_ready, it * BUFS + u + 1)
                    act.activation(std[:, u, :], mv[:, u, :, 1], ACT.Sqrt, bias=eps[:]).then_inc(std_ready, 1)

            act.wait_ge(consts, 1)
            run(0)
            if ROUNDS > 1:
                with act.Fori(1, ROUNDS) as it:
                    run(it)
            finish(ROUNDS - 1, BUFS - 1)

        @block.vector
        def _(dve):
            PER = 6
            with dve.Fori(0, ROUNDS) as it:
                for u in range(BUFS):
                    n = BUFS * it + u
                    done = n * PER
                    gsum = acc[:, u, :, D]
                    dve.wait_ge(a_in[u], 32 * (it + 1))
                    dve.tensor_scalar(sums[:, 0], gsum, 0.0, None, ALU.is_gt).then_inc(d, 1)
                    dve.wait_ge(d, done + 1)
                    dve.tensor_scalar(sums[:, 1], sums[:, 0], -1.0, 1.0, ALU.mult, ALU.add).then_inc(d, 1)
                    dve.wait_ge(d, done + 2)
                    dve.tensor_tensor(sums[:, 2], sums[:, 1], gsum, ALU.add).then_inc(d, 1)
                    dve.wait_ge(d, done + 3)
                    dve.reciprocal(sums[:, 3], sums[:, 2]).then_inc(d, 1)
                    dve.wait_ge(d, done + 4)
                    for t in range(QT):
                        ins = dve.scalar_tensor_tensor(out=z[:, u, t, :], in0=acc[:, u, t, 0:D],
                                                       scalar=sums[:, 3, t:t + 1], in1=z[:, u, t, :],
                                                       op0=ALU.mult, op1=ALU.add)
                    ins.then_inc(d, 1)
                    dve.wait_ge(d, done + 5)
                    for t in range(QT):
                        ins = dve.bn_stats(stats[:, t, :], z[:, u, t, :])
                    ins.then_inc(d, 1)
                    plain(dve, d, done + 6, passed)
                    for t in range(QT):
                        ins = dve.bn_aggr(mv[:, u, t, :], stats[:, t, :])
                    ins.then_inc(mv_ready, 1)
                    dve.wait_ge(std_ready, n + 1)
                    dve.reciprocal(rstd[:, u], std[:, u, :]).then_inc(rstd_ready, 1)
                    dve.wait_ge(rstd_ready, n + 1)
                    dve.scalar_tensor_tensor(out=shift[:, u], in0=mv[:, u, :, 0], scalar=-1.0, in1=rstd[:, u],
                                             op0=ALU.mult, op1=ALU.mult).then_inc(shift_ready, 1)


def build_program(nc, x, xT, w, out, NB):
    N = NB * T
    scratch = {"wqk": nc.dram_tensor("scratch_wqk", [GROUPS, P, 4 * DC * P], F32).ap()}
    x1_dram = nc.dram_tensor("scratch_x1", [N, D], F32).ap()
    table = nc.dram_tensor("scratch_table", [N, TABLE], F32).ap()
    acc_dram = nc.dram_tensor("scratch_sums", [N, ACC], F32).ap()
    logits_dram = nc.dram_tensor("scratch_logits", [E_N, N], F32).ap()
    list_dram = nc.dram_tensor("scratch_lists", [E_N, N // E_N], U32).ap()
    with ExitStack() as ctx:
        sb = lambda name, shape, dt=F32: ctx.enter_context(nc.sbuf_tensor(name, shape, dt))
        keep = {"wo": sb("wo_cols", [P, DC, D]), "wv": sb("wv_parts", [P, 2, DC, D], F32R),
                "bq": sb("bq_folded", [P, GROUPS]), "bk": sb("bk_cols", [P, GROUPS]), "bo": sb("bo_folded", [P, D])}
        build_weights(nc, w, scratch, keep)
        build_attention(nc, x, xT, x1_dram, acc_dram, scratch, keep, NB)
    with ExitStack() as ctx:
        logits = ctx.enter_context(nc.sbuf_tensor("logits_t", [E_N, N], F32))
        build_router(nc, x1_dram, w, table, logits_dram, logits, NB)
        build_selection(nc, table, logits_dram, list_dram, logits, NB)
    build_experts(nc, w, table, list_dram, acc_dram, NB)
    build_final(nc, x1_dram, acc_dram, out, NB)


def kernel(**inputs):
    import concourse.bacc as _bacc
    from concourse.bass_utils import run_bass_kernel_spmd as _run

    attn = lambda name: np.asarray(inputs["L0_attn_" + name])
    ffn = lambda name: np.asarray(inputs["L0_ffn_" + name])
    B, S, _ = attn("x").shape
    x = attn("x").reshape(B * S, D)
    layout = {
        "x": x, "xT": x.T,
        "Wq": attn("Wq"), "WkT": attn("Wk").T, "WvT": attn("Wv").T, "WoT": attn("Wo").T,
        "bq": attn("bq"), "bk": attn("bk"), "bv": attn("bv"), "bo": attn("bo"),
        "LqT": attn("Wq_lsr").transpose(0, 2, 1), "LkT": attn("Wk_lsr").transpose(0, 2, 1),
        "norm": ffn("norm_weight"), "rwT": ffn("router_weight").T, "rb": ffn("router_bias"),
        "w1T": ffn("fc1_weight").transpose(0, 2, 1), "w2T": ffn("fc2_weight").transpose(0, 2, 1),
        "b1T": ffn("fc1_bias").reshape(E_N, FC, P).transpose(0, 2, 1), "b2": ffn("fc2_bias"),
    }
    nc = _bacc.Bacc("TRN2", target_bir_lowering=False, num_devices=1)
    arrays = {"in_" + k: np.ascontiguousarray(a) for k, a in layout.items()}
    w = {k: nc.dram_tensor("in_" + k, arrays["in_" + k].shape, mybir.dt.from_np(arrays["in_" + k].dtype),
                           kind="ExternalInput").ap() for k in layout}
    out = nc.dram_tensor("out_x", (B * S, D), F32, kind="ExternalOutput").ap()
    build_program(nc, w["x"], w["xT"], w, out, B)
    r = _run(nc, [arrays], core_ids=[0])
    return r.results[0]["out_x"].reshape(B, S, D)
```
